# Optimizing a Trainium2 kernel written in Bass

```python
import numpy as np
import jax
import jax.numpy as jnp

def _softmax(x, axis=-1):
    return jax.nn.softmax(x, axis=axis)
def _gelu(x):
    return jax.nn.gelu(x, approximate=True)
def _silu(x):
    return jax.nn.silu(x)
def _sigmoid(x):
    return jax.nn.sigmoid(x)
def _layernorm(x, axis=-1, eps=1e-5):
    m = jnp.mean(x, axis=axis, keepdims=True)
    v = jnp.var(x, axis=axis, keepdims=True)
    return (x - m) / jnp.sqrt(v + eps)
def _scatter_add(tgt, idx, src, axis=0):
    return tgt.at[idx].add(src)
def _segment_sum(src, seg, n):
    return jax.ops.segment_sum(src, seg, n)

kernel_name = 'mk_adj_resnorm_d2_adj_256_4e2169'

def setup_inputs(seed: int = 0):
    np.random.seed(seed)
    _w = jnp.asarray
    def _rec_inputs():
        import jax
        import jax.numpy as jnp
        _gk = jax.random.key(seed)
        x = -0.0005146 + 1 * jax.random.normal(jax.random.fold_in(_gk, 1), (8, 2048, 256), jnp.float32)
        _a = jax.random.bernoulli(jax.random.fold_in(_gk, 2), 0.0078125, (8, 2048, 2048))
        _a = jnp.logical_or(_a, jnp.swapaxes(_a, -1, -2))
        _a = jnp.logical_or(_a, jnp.eye(2048, dtype=bool))
        adj = _a.astype(jnp.int32)
        return x, adj
    x, adj = _rec_inputs()
    def _L0_gnn_setup():
        import jax, jax.numpy as jnp
        import numpy as np
        B, N, C, OUT, S = (4, 2048, 256, 256, 25)
        DENSITY = 0.008
        key = jax.random.key(seed)
        kA, kX, kW = jax.random.split(key, 3)
        A = jax.random.bernoulli(kA, DENSITY, (B, N, N)).astype(jnp.int32)
        X = jax.random.normal(kX, (B, N, C), dtype=jnp.float32)
        W = jax.random.normal(kW, (2 * C, OUT), dtype=jnp.float32) * np.float32(1.0 / np.sqrt(2 * C))
        b = jnp.zeros((OUT,), dtype=jnp.float32)
        return {'A': A, 'X': X, 'W': W, 'b': b}
    _L0_gnn_all = _L0_gnn_setup()
    _L0_gnn_in = {k: v for k, v in _L0_gnn_all.items() if k in ('W', 'b', )}
    del _L0_gnn_all

    def _L1_gnn_setup():
        import jax, jax.numpy as jnp
        import numpy as np
        B, N, D = (8, 1024, 256)
        H, HO = (4, 64)
        T = 5
        NEG = -1000000000.0
        EPS = 1e-06
        key = jax.random.key(seed)
        ks = jax.random.split(key, 6)
        nodes_embed = jax.random.normal(ks[0], (B, N, D), dtype=jnp.float32)
        node_adj = jax.random.randint(ks[1], (B, N, N), 0, T + 1)
        W = jax.random.normal(ks[2], (H, D, HO), dtype=jnp.float32) * (1.0 / np.sqrt(D))
        a_src = jax.random.normal(ks[3], (H, T, HO), dtype=jnp.float32) * 0.1
        a_dst = jax.random.normal(ks[4], (H, T, HO), dtype=jnp.float32) * 0.1
        bias = jnp.zeros((H, HO), dtype=jnp.float32)
        ln_gamma = jnp.ones((H, HO), dtype=jnp.float32)
        ln_beta = jnp.zeros((H, HO), dtype=jnp.float32)
        return {'nodes_embed': nodes_embed, 'node_adj': node_adj, 'W': W, 'a_src': a_src, 'a_dst': a_dst, 'bias': bias, 'ln_gamma': ln_gamma, 'ln_beta': ln_beta}
    _L1_gnn_all = _L1_gnn_setup()
    _L1_gnn_in = {k: v for k, v in _L1_gnn_all.items() if k in ('W', 'a_src', 'a_dst', 'bias', 'ln_gamma', 'ln_beta', )}
    del _L1_gnn_all

    return {
        "x": x,
        "adj": adj,
        "L0_gnn_W": _L0_gnn_in["W"],
        "L0_gnn_b": _L0_gnn_in["b"],
        "L1_gnn_W": _L1_gnn_in["W"],
        "L1_gnn_a_src": _L1_gnn_in["a_src"],
        "L1_gnn_a_dst": _L1_gnn_in["a_dst"],
        "L1_gnn_bias": _L1_gnn_in["bias"],
        "L1_gnn_ln_gamma": _L1_gnn_in["ln_gamma"],
        "L1_gnn_ln_beta": _L1_gnn_in["ln_beta"],
    }

def reference(x, adj, L0_gnn_W, L0_gnn_b, L1_gnn_W, L1_gnn_a_src, L1_gnn_a_dst, L1_gnn_bias, L1_gnn_ln_gamma, L1_gnn_ln_beta):
    import jax
    import jax.numpy as jnp
    def _L0_gnn_ref(A, X, W, b):
        import jax, jax.numpy as jnp
        import numpy as np
        B, N, C, OUT, S = (4, 2048, 256, 256, 25)
        DENSITY = 0.008
        mask = A != 0
        neg_inf = jnp.float32(-jnp.inf)
        pri = -jnp.arange(N, dtype=jnp.float32)
        scores = jnp.where(mask, pri, neg_inf)
        vals, idx = jax.lax.top_k(scores, S)
        valid = vals > neg_inf
        feats = jax.vmap(lambda x, i: x[i])(X, idx)
        feats = jnp.where(valid[..., None], feats, neg_inf)
        agg = feats.max(axis=2)
        degree = mask.sum(axis=-1)
        agg = jnp.where((degree <= S)[..., None], jnp.maximum(agg, 0.0), agg)
        h = jnp.concatenate([X, agg], axis=-1)
        out = jax.nn.relu(jnp.einsum('bnf,fo->bno', h, W) + b)
        return out

    def _L1_gnn_ref(nodes_embed, node_adj, W, a_src, a_dst, bias, ln_gamma, ln_beta):
        import jax, jax.numpy as jnp
        import numpy as np
        B, N, D = (8, 1024, 256)
        H, HO = (4, 64)
        T = 5
        NEG = -1000000000.0
        EPS = 1e-06
        h = jnp.einsum('bnd,hde->bhne', nodes_embed, W)
        e_src = jnp.einsum('bhne,hte->bhtn', h, a_src)
        e_dst = jnp.einsum('bhne,hte->bhtn', h, a_dst)
        n_types = a_src.shape[1]
        weight = jnp.zeros(h.shape[:2] + (h.shape[2], h.shape[2]), dtype=h.dtype)
        for t in range(n_types):
            mask = (node_adj == t + 1).astype(h.dtype)[:, None]
            weight = weight + mask * (e_src[:, :, t, :, None] + e_dst[:, :, t, None, :])
        weight = jax.nn.leaky_relu(weight, negative_slope=0.01)
        weight = jnp.where(node_adj[:, None] == 0, NEG, weight)
        attention = jax.nn.softmax(weight, axis=-1)
        dst = jnp.einsum('bhij,bhje->bhie', attention, h) + bias[None, :, None, :]
        out = jax.nn.relu(dst) + h
        mu = out.mean(axis=-1, keepdims=True)
        var = out.var(axis=-1, keepdims=True)
        out = (out - mu) / jnp.sqrt(var + EPS) * ln_gamma[None, :, None, :] + ln_beta[None, :, None, :]
        b, hh, n, e = out.shape
        return out.transpose(0, 2, 1, 3).reshape(b, n, hh * e)

    x = _layernorm(x + _L0_gnn_ref(adj, x, L0_gnn_W, L0_gnn_b), axis=-1)
    x = _layernorm(x + _L1_gnn_ref(x, adj, L1_gnn_W, L1_gnn_a_src, L1_gnn_a_dst, L1_gnn_bias, L1_gnn_ln_gamma, L1_gnn_ln_beta), axis=-1)
    return x


_drawn_inputs = setup_inputs


def setup_inputs(seed=0):
    import zlib

    import numpy as np

    out = dict(_drawn_inputs(seed))
    spreads = {'L0_gnn_b': (0.0, 0.1),
     'L1_gnn_bias': (0.0, 0.1),
     'L1_gnn_ln_gamma': (1.0, 0.2),
     'L1_gnn_ln_beta': (0.0, 0.1)}
    factors = {'L1_gnn_a_src': 3.118}
    for name, (base, spread) in spreads.items():
        noise = np.random.default_rng([zlib.crc32(name.encode()), seed]).standard_normal(out[name].shape)
        drawn = base * np.exp(spread * noise) if base else spread * noise
        out[name] = jnp.asarray(drawn.astype(out[name].dtype))
    for name, factor in factors.items():
        out[name] = (out[name] * factor).astype(out[name].dtype)
    return out
```

```python
from contextlib import ExitStack

import concourse.bass as bass
from concourse import mybir

ALU = mybir.AluOpType
ACT = mybir.ActivationFunctionType
AX = mybir.AxisListType
F32 = mybir.dt.float32
F16 = mybir.dt.float16
BF16 = mybir.dt.bfloat16
I32 = mybir.dt.int32
U32 = mybir.dt.uint32
U8 = mybir.dt.uint8

P = 128
B, N, C = 8, 2048, 256
HEADS, HO = 4, 64
HW = HO + 1
S = 25
JT = N // P
TILES = B * JT
QT = 4
IB = QT * P
QUADS = TILES // QT
BQ = JT // QT
RING = 6
WORD = 16
WORDS = N // WORD
WPT = P // WORD
NIB = 4
TOP = 32
CH = 5
CR = S // CH
HALF = JT // 2
UNITS = JT * 2
UVB = 4
BIG = 3.0e38
FIN = QT * (BQ + 1)
CHUNK_AFTER = [0, 2, 4, 5, 7]
LN0_EPS = 1e-5
HEAD_EPS = 1e-6
LEAK = 0.01


class Quad:

    def __init__(self, eng, q, first, last):
        self.eng, self.q, self.first, self.last = eng, q, first, last

    def on(self, u, lag):
        here = [0 <= QT * q + u - lag < TILES for q in (self.first, self.last)]
        assert here[0] == here[1]
        return here[0]

    def wait(self, sem, count):
        if count(self.last) <= 0:
            return
        assert count(self.first) > 0
        self.eng.wait_ge(sem, count(self.q))


def run_quads(eng, step):
    def quad(q, first, last):
        for u in range(QT):
            step(Quad(eng, q, first, last), u)

    for a, b in ((0, 1), (1, BQ), (BQ, BQ + 1), (BQ + 1, BQ + 2), (BQ + 2, QUADS - 1), (QUADS - 1, QUADS),
                 (QUADS, QUADS + 1), (QUADS + 1, QUADS + BQ), (QUADS + BQ, QUADS + BQ + 1),
                 (QUADS + BQ + 1, QUADS + BQ + 2)):
        if b == a + 1:
            quad(a, a, a)
        else:
            with eng.Fori(a, b) as q:
                quad(q, a, b - 1)


def projected(quad, u):
    return QT * quad.q + u - 1 if QT * quad.first + u <= TILES + 1 else TILES


def after(quad, u, ahead):
    return quad.q + (u + ahead) // QT, (u + ahead) % QT


class Chain:

    def __init__(self, eng, sem):
        self.eng, self.sem, self.n = eng, sem, 0

    def then(self, instruction):
        self.n += 1
        instruction.then_inc(self.sem, 1)
        self.eng.wait_ge(self.sem, self.n)

    def end(self):
        self.eng.sem_clear(self.sem)


def layers_program(nc, x, adj, w0, b0, w1, a_src, a_dst, bias1, gamma, beta,
                   c_id16, c_id32, c_pack, c_wordkey, c_nib, c_mask, c_col, c_sel, c_base, out):
    x_rows = x.rearrange("b n c -> (b n) c")
    adj_rows = adj.rearrange("b n m -> (b n) m")
    out_rows = out.rearrange("b n c -> (b n) c")
    x1_dram = nc.dram_tensor("x1_dram", (B * N, C), F32).ap()

    ctx = ExitStack()
    with ctx:
        def sb(name, shape, dt):
            return ctx.enter_context(nc.sbuf_tensor(name, shape, dt))

        def ps(name, shape, dt):
            return ctx.enter_context(nc.psum_tensor(name, shape, dt))

        def sem(name):
            return ctx.enter_context(nc.semaphore(name))

        id16 = sb("id16", [P, P], F16)
        id32 = sb("id32", [P, P], F32)
        pack = sb("pack", [P, WPT], BF16)
        wordkey = sb("wordkey", [P, WORDS], F32)
        nibkey = sb("nibkey", [P, NIB], F32)
        bitmask = sb("bitmask", [P, NIB], I32)
        colkey = sb("colkey", [P, NIB], F32)
        sel = sb("sel", [HEADS, HEADS, P], F32)
        w0_sb = sb("w0_sb", [P, 4, C], F32)
        b0_sb = sb("b0_sb", [1, C], F32)
        ones_row = sb("ones_row", [1, P], F32)
        wcat = sb("wcat", [P, 2, C + 2 * HEADS], F32)
        bias_b = sb("bias_b", [P, C], F32)
        gamma_b = sb("gamma_b", [P, C], F32)
        beta_b = sb("beta_b", [P, C], F32)
        eps0 = sb("eps0", [P, 1], F32)
        eps1 = sb("eps1", [P, 1], F32)
        rowbase = sb("rowbase", [P, TILES], F32)
        adj_sb = sb("adj_sb", [P, N], I32)
        mask_sb = sb("mask_sb", [P, N], F16)
        stage = sb("stage", [P, JT, P], BF16)
        maskT = sb("maskT", [P, RING * JT, IB], U8)
        key_a = sb("key_a", [P, WORDS], F32)
        key_b = sb("key_b", [P, WORDS], F32)
        top = sb("top", [P, TOP], F32)
        topi = sb("topi", [P, TOP], I32)
        part = sb("part", [P, TOP, NIB], I32)
        high = sb("high", [P, TOP], I32)
        value = sb("value", [P, TOP, NIB], F32)
        pad = sb("pad", [P, S], F32)
        lim = [sb(f"lim{p}", [P, 2], F32) for p in range(2)]
        idx = [sb(f"idx{p}", [P, S], U32) for p in range(2)]
        rows = sb("rows", [P, CH, CR * C], F32)
        cmax = sb("cmax", [P, CH, C], F32)
        agg = sb("agg", [P, C], F32)
        xt = [sb(f"xt{p}", [P, C], F32) for p in range(2)]
        xaT = sb("xaT", [P, 4, P], F32)
        r0 = sb("r0", [P, C], F32)
        st0 = sb("st0", [P, 6], F32)
        mv0 = sb("mv0", [P, 2], F32)
        sd0 = sb("sd0", [P, 1], F32)
        rs0 = sb("rs0", [P, 1], F32)
        x1 = [sb(f"x1_{p}", [P, C], F32) for p in range(2)]
        x1T = sb("x1T", [P, 2, P], F32)
        hs = sb("hs", [P, 2 * JT, HEADS, HW], F32)
        esT = sb("esT", [HEADS, RING * IB], F32)
        bj = sb("bj", [P, 2 * JT, HEADS], F32)
        dj = sb("dj", [P, 2 * JT, HEADS], F32)
        ndj = sb("ndj", [P, 2 * JT, HEADS], F32)
        rb = sb("rb", [P, HEADS, IB], F32)
        uv = [sb(f"uv{k}", [P, 2, IB], F32) for k in range(UVB)]
        rden = sb("rden", [P, QT, HEADS], F32)
        dst = sb("dst", [P, QT, C], F32)
        x1r = [sb(f"x1r{p}", [P, C], F32) for p in range(2)]
        oh = sb("oh", [P, C], F32)
        sth = sb("sth", [P, HEADS, 6], F32)
        mvh = sb("mvh", [P, HEADS, 2], F32)
        sdh = sb("sdh", [P, HEADS], F32)
        rsh = sb("rsh", [P, HEADS], F32)
        stf = sb("stf", [P, 6], F32)
        mvf = sb("mvf", [P, 2], F32)
        r1 = sb("r1", [P, 1], F32)
        sdf = sb("sdf", [P, 1], F32)
        rsf = sb("rsf", [P, 1], F32)
        outb = [sb(f"outb{p}", [P, C], F32) for p in range(2)]

        acc = [ps(f"acc{i}", [P, 512], F32) for i in range(QT)]
        pT = [ps(f"pT{i}", [P, HALF * P], F16) for i in range(2)]
        pA = ps("pA", [P, 512], F32)
        pB = ps("pB", [P, 512], F32)
        p_lin, p_key = pB[:, 0:C], pB[:, 384:384 + WORDS]
        p_h = pB[:, 0:C + 2 * HEADS]
        p_x1T, p_es = pA[:, 0:2 * P], pA[0:HEADS, 2 * P:3 * P]

        s_const = sem("s_const")
        s_go_pool = sem("s_go_pool")
        s_go_pe = sem("s_go_pe")
        s_setup = sem("s_setup")
        s_wa = sem("s_wa")
        s_adj = sem("s_adj")
        s_x = [sem(f"s_xin{p}") for p in range(2)]
        s_mask = sem("s_mask")
        s_T = sem("s_T")
        s_stage = sem("s_stage")
        s_ring = sem("s_ring")
        s_key = sem("s_key")
        s_keyread = sem("s_keyread")
        s_topk = sem("s_topk")
        s_idx = sem("s_idx")
        s_rows = [sem(f"s_rows{c}") for c in range(CH)]
        s_rfree = sem("s_rfree")
        s_maxc = sem("s_maxc")
        s_agg = sem("s_agg")
        s_xaT = sem("s_xaT")
        s_xaE = sem("s_xaE")
        s_lin = sem("s_lin")
        s_r0 = sem("s_r0")
        s_late = sem("s_late")
        s_mv0 = sem("s_mv0")
        s_sd0 = sem("s_sd0")
        s_x1 = sem("s_x1")
        s_x1st = [sem(f"s_x1store{p}") for p in range(2)]
        s_x1T = sem("s_x1T")
        s_x1E = sem("s_x1E")
        s_h = sem("s_h")
        s_proj = sem("s_proj")
        s_ed = sem("s_ed")
        s_es = sem("s_es")
        s_rb = sem("s_rb")
        s_v = sem("s_v")
        s_u = sem("s_u")
        s_pe = sem("s_pe")
        s_blk = sem("s_blk")
        s_accfree = sem("s_accfree")
        s_norm = sem("s_norm")
        s_x1r = [sem(f"s_x1load{p}") for p in range(2)]
        s_fin = sem("s_fin")
        s_mvh = sem("s_mvh")
        s_sdh = sem("s_sdh")
        s_mvf = sem("s_mvf")
        s_sdf = sem("s_sdf")
        s_out = sem("s_out")
        s_st = [sem(f"s_st{p}") for p in range(2)]

        consts = [(id16[:], c_id16), (id32[:], c_id32), (pack[:], c_pack), (wordkey[:], c_wordkey),
                  (nibkey[:], c_nib), (bitmask[:], c_mask), (colkey[:], c_col), (sel[:], c_sel),
                  (w0_sb[:], w0.rearrange("(c p) o -> p c o", p=P)),
                  (b0_sb[:], b0.rearrange("(a n) -> a n", a=1)),
                  (bias_b[:], bias1.rearrange("h e -> (h e)").partition_broadcast(P)),
                  (gamma_b[:], gamma.rearrange("h e -> (h e)").partition_broadcast(P)),
                  (beta_b[:], beta.rearrange("h e -> (h e)").partition_broadcast(P)),
                  (rowbase[:], c_base),
                  (dst[:, 0, :].rearrange("p (h e) -> p h e", h=HEADS), a_src[:, 0, :].partition_broadcast(P)),
                  (dst[:, 1, :].rearrange("p (h e) -> p h e", h=HEADS), a_dst[:, 0, :].partition_broadcast(P)),
                  (wcat[:, 0, 0:C].rearrange("p (h e) -> p h e", h=HEADS), w1.rearrange("h (c p) e -> p c h e", p=P)[:, 0]),
                  (wcat[:, 1, 0:C].rearrange("p (h e) -> p h e", h=HEADS), w1.rearrange("h (c p) e -> p c h e", p=P)[:, 1])]
        CONST = 16 * len(consts)


        block = ctx.enter_context(nc.Block())

        @block.sync
        def _(sp):
            for dst_ap, src in consts:
                sp.dma_start(dst_ap, src).then_inc(s_const, 16)
            sp.dma_start(adj_sb[:], adj_rows[0:P, :]).then_inc(s_adj, 16)

            def step(quad, u):
                s, p = QT * quad.q + u, u % 2
                if quad.on(u, -1):
                    quad.wait(s_mask, lambda q: QT * q + u + 1)
                    sp.dma_start(adj_sb[:], adj_rows[bass.ds((s + 1) * P, P), :]).then_inc(s_adj, 16)
                if quad.on(u, 0):
                    quad.wait(s_r0, lambda q: QT * q + u - 1)
                    sp.dma_start(xt[p][:], x_rows[bass.ds(s * P, P), :]).then_inc(s_x[p], 16)
                if quad.on(u, 2):
                    quad.wait(s_x1, lambda q: QT * q + u - 1)
                    sp.dma_start(x1_dram[bass.ds((s - 2) * P, P), :], x1[p][:]).then_inc(s_x1st[p], 16)
                if quad.on(u, FIN):
                    quad.wait(s_out, lambda q: QT * q + u - FIN - 1)
                    quad.wait(s_x1st[p], lambda q: 16 * (2 * q + (u - FIN) // 2 + 1))
                    sp.dma_start(x1r[p][:], x1_dram[bass.ds((s - FIN) * P, P), :]).then_inc(s_x1r[p], 16)
                if quad.on(u, FIN + 1):
                    quad.wait(s_out, lambda q: QT * q + u - FIN)
                    sp.dma_start(out_rows[bass.ds((s - FIN - 1) * P, P), :], outb[1 - p][:]).then_inc(s_st[1 - p], 16)

            run_quads(sp, step)
            for p in range(2):
                sp.wait_ge(s_st[p], 16 * TILES // 2)
                sp.wait_ge(s_x1st[p], 16 * TILES // 2)

        @block.gpsimd
        def _(pool):
            def step(quad, u):
                if not quad.on(u, 0):
                    return
                p = u % 2
                quad.wait(s_idx, lambda q: QT * q + u + 1)
                for c in range(CH):
                    quad.wait(s_rfree, lambda q: CH * (QT * q + u) + c + 1)
                    pool.sem_inc(s_go_pool, 1)
                    for r in range(CR):
                        k = c * CR + r
                        nc.gpsimd.indirect_dma_start(
                            rows[:, c, r * C:(r + 1) * C], None, x_rows,
                            bass.IndirectOffsetOnAxis(ap=idx[p][:, k:k + 1], axis=0)).then_inc(s_rows[c], 16)

            run_quads(pool, step)

        @block.scalar
        def _(act):
            act.wait_ge(s_const, CONST)
            act.wait_ge(s_setup, 1)

            def transposed(quad, u, g_of):
                qg, ug = after(quad, u, g_of)
                for hf in range(2):
                    quad.wait(s_T, lambda q: 2 * (QT * q + u + g_of) + hf + 1)
                    quad.wait(s_key, lambda q: QT * q + u + g_of)
                    src = pT[hf][:, :].rearrange("p (j i) -> p j i", i=P)
                    nc.scalar.activation(stage[:, hf * HALF:(hf + 1) * HALF, :], src, ACT.Copy).then_inc(s_stage, 1)
                    quad.wait(s_blk, lambda q: q + (u + g_of) // QT + 1)
                    nc.scalar.activation(maskT[:, bass.ds(qg % RING * JT + hf * HALF, HALF), ug * P:(ug + 1) * P],
                                         src, ACT.Copy).then_inc(s_ring, 1)

            def relu_units(quad, u, part):
                par = (quad.q - BQ) // BQ % 2 * JT
                for n in range(part * 4, part * 4 + 4):
                    jt, hh, k = QT * u + n // 2, n % 2, n % UVB
                    quad.wait(s_pe, lambda q: UNITS * (q - BQ) + 8 * u + n - UVB + 1)
                    for i in range(2):
                        h = 2 * hh + i
                        last = nc.scalar.activation(uv[k][:, i, :], rb[:, h, :], ACT.Relu,
                                                    bias=ndj[:, bass.ds(par + jt, 1), h], scale=bj[:, bass.ds(par + jt, 1), h])
                    last.then_inc(s_v, 1)

            def step(quad, u):
                s, p = QT * quad.q + u, u % 2
                if quad.on(u, -1):
                    transposed(quad, u, 1)
                att = quad.on(u, QT * BQ)
                if att and u == 0:
                    for h in range(HEADS):
                        quad.wait(s_es, lambda q: HEADS * (q - BQ) + h + 1)
                        nc.scalar.activation(rb[:, h, :], pA[:, :], ACT.Exp, scale=1.0 - LEAK).then_inc(s_rb, 1)
                    act.wait_ge(s_rb, HEADS * (quad.q - BQ + 1))
                if quad.on(u, 1):
                    quad.wait(s_xaT, lambda q: QT * q + u)
                    quad.wait(s_lin, lambda q: QT * q + u - 1)
                    nc.scalar.activation(xaT[:, :, :], pA[:, :].rearrange("p (c i) -> p c i", c=4), ACT.Copy).then_inc(s_xaE, 1)
                if att:
                    act.wait_ge(s_proj, projected(quad, u))
                    relu_units(quad, u, 0)
                if quad.on(u, 1):
                    quad.wait(s_mv0, lambda q: QT * q + u)
                    nc.scalar.activation(sd0[:], mv0[:, 1:2], ACT.Sqrt, bias=eps0[:]).then_inc(s_sd0, 1)
                if att:
                    relu_units(quad, u, 1)
                if quad.on(u, 1):
                    project(quad, u)
                if quad.on(u, FIN):
                    quad.wait(s_mvh, lambda q: QT * q + u - FIN + 1)
                    nc.scalar.activation(sdh[:, :], mvh[:, :, 1], ACT.Sqrt, bias=eps1[:]).then_inc(s_sdh, 1)
                    quad.wait(s_mvf, lambda q: QT * q + u - FIN + 1)
                    nc.scalar.activation(sdf[:], mvf[:, 1:2], ACT.Sqrt, bias=eps0[:]).then_inc(s_sdf, 1)

            def project(quad, u):
                qg, ug = after(quad, u, -1)
                quad.wait(s_x1T, lambda q: QT * q + u)
                nc.scalar.activation(x1T[:, :, :], p_x1T.rearrange("p (c i) -> p c i", c=2), ACT.Copy).then_inc(s_x1E, 1)
                quad.wait(s_h, lambda q: QT * q + u)
                quad.wait(s_pe, lambda q: UNITS * (q + (u - 1) // QT - BQ))
                t = qg // BQ % 2 * JT + qg % BQ * QT + ug
                hcopy = nc.scalar.activation(hs[:, bass.ds(t, 1), :, 0:HO],
                                             pB[:, 0:C].rearrange("p (t h e) -> p t h e", t=1, h=HEADS), ACT.Copy)
                hcopy.then_inc(s_ed, 1)
                nc.scalar.activation(esT[:, bass.ds(qg % RING * IB + ug * P, P)], p_es, ACT.Copy).then_inc(s_ed, 1)
                ed = pB[:, C + HEADS:C + 2 * HEADS]
                nc.scalar.activation(bj[:, bass.ds(t, 1), :], ed.unsqueeze(1), ACT.Exp).then_inc(s_ed, 1)
                nc.scalar.activation(dj[:, bass.ds(t, 1), :], ed.unsqueeze(1), ACT.Exp, scale=LEAK).then_inc(s_ed, 1)
                quad.wait(s_ed, lambda q: 4 * (QT * q + u))
                nc.scalar.activation(ndj[:, bass.ds(t, 1), :], dj[:, bass.ds(t, 1), :], ACT.Copy, scale=-1.0).then_inc(s_proj, 1)

            quad0 = Quad(act, 0, 0, 0)
            transposed(quad0, 0, 0)
            run_quads(act, step)

        @block.vector
        def _(dve):
            for t in range(2 * JT):
                nc.vector.memset(hs[:, t, :, HO:HW], 1.0)
            nc.vector.memset(ones_row[:], 1.0)
            nc.vector.memset(eps0[:], LN0_EPS)
            nc.vector.memset(eps1[:], HEAD_EPS).then_inc(s_rfree, CH)
            dve.wait_ge(s_const, CONST)
            for c in range(2):
                for k in range(2):
                    nc.vector.tensor_tensor(r0[:], wcat[:, c, 0:C], dst[:, k, :], ALU.mult).then_inc(s_wa, 1)
                    dve.wait_ge(s_wa, 4 * c + 2 * k + 1)
                    nc.vector.tensor_reduce(wcat[:, c, C + HEADS * k:C + HEADS * (k + 1)],
                                            r0[:].rearrange("p (h e) -> p h e", h=HEADS), axis=AX.X, op=ALU.add).then_inc(s_wa, 1)
                    dve.wait_ge(s_wa, 4 * c + 2 * k + 2)
            nc.vector.memset(r0[:, 0:1], 0.0).then_inc(s_blk, RING)
            nc.vector.memset(r0[:, 1:2], 0.0).then_inc(s_setup, 1)

            def top32(ch):
                a, b = key_a, key_b
                for k in range(0, TOP, 8):
                    ch.then(nc.vector.max(top[:, k:k + 8], a[:]))
                    if k + 8 < TOP:
                        ch.then(nc.vector.match_replace(b[:], top[:, k:k + 8], a[:], 0.0))
                        a, b = b, a

            def early(quad, u, g_of):
                p = (u + g_of) % 2
                g = QT * quad.q + u + g_of
                quad.wait(s_adj, lambda q: 16 * (QT * q + u + g_of + 1))
                quad.wait(s_T, lambda q: 2 * (QT * q + u + g_of))
                nc.vector.tensor_scalar(mask_sb[:], adj_sb[:], 0.0, None, ALU.not_equal).then_inc(s_mask, 1)
                quad.wait(s_key, lambda q: QT * q + u + g_of + 1)
                ch = Chain(dve, s_topk)
                ch.then(nc.vector.scalar_tensor_tensor(key_b[:], p_key, 0.0, wordkey[:], ALU.is_gt, ALU.mult))
                ch.then(nc.vector.tensor_tensor(key_a[:], p_key, key_b[:], ALU.add))
                nc.vector.memset(pad[:, 0:1], 0.0).then_inc(s_keyread, 1)
                top32(ch)
                ch.then(nc.vector.tensor_copy(topi[:], top[:]))
                nc.vector.tensor_scalar(high[:], topi[:], 10, (WORDS - 1) << 6, ALU.logical_shift_right, ALU.bitwise_and)
                for n in range(NIB):
                    last = nc.vector.tensor_scalar(part[:, :, n], topi[:], WORD - NIB * (n + 1), 15,
                                                   ALU.logical_shift_right, ALU.bitwise_and)
                ch.then(last)
                a3, b3 = (k[:].rearrange("p (t n) -> p t n", n=NIB) for k in (key_a, key_b))
                ch.then(nc.vector.tensor_tensor(value[:], high[:].unsqueeze(2).to_broadcast([P, TOP, NIB]),
                                                nibkey[:].unsqueeze(1).to_broadcast([P, TOP, NIB]), ALU.add))
                ch.then(nc.vector.scalar_tensor_tensor(b3, part[:], 0.0, value[:], ALU.is_gt, ALU.mult))
                ch.then(nc.vector.tensor_tensor(a3, part[:], b3, ALU.add))
                top32(ch)
                ch.then(nc.vector.tensor_copy(topi[:], top[:]))
                nc.vector.tensor_scalar(high[:], topi[:], 2, N - NIB, ALU.logical_shift_right, ALU.bitwise_and)
                ch.then(nc.vector.tensor_tensor(part[:], topi[:].unsqueeze(2).to_broadcast([P, TOP, NIB]),
                                                bitmask[:].unsqueeze(1).to_broadcast([P, TOP, NIB]), ALU.bitwise_and))
                ch.then(nc.vector.tensor_tensor(value[:], high[:].unsqueeze(2).to_broadcast([P, TOP, NIB]),
                                                colkey[:].unsqueeze(1).to_broadcast([P, TOP, NIB]), ALU.add))
                ch.then(nc.vector.scalar_tensor_tensor(a3, part[:], 0.0, value[:], ALU.is_gt, ALU.mult))
                top32(ch)
                nc.vector.tensor_scalar(lim[p][:, 0:1], top[:, S:S + 1], 0.0, -BIG, ALU.is_gt, ALU.mult)
                nc.vector.tensor_scalar(lim[p][:, 1:2], top[:, 0:1], 0.0, BIG, ALU.is_gt, ALU.mult)
                ch.then(nc.vector.tensor_scalar(pad[:], top[:, 0:S], 0.0, top[:, 0:1], ALU.is_equal, ALU.mult))
                ch.then(nc.vector.tensor_tensor(pad[:], pad[:], top[:, 0:S], ALU.add))
                ch.then(nc.vector.tensor_scalar(pad[:], pad[:], 1.0, -1.0, ALU.max, ALU.mult))
                ch.then(nc.vector.tensor_scalar(idx[p][:], pad[:], rowbase[:, bass.ds(g, 1)], None, ALU.add))
                nc.vector.memset(pad[:, 0:1], 0.0).then_inc(s_idx, 1)
                ch.end()

            def late(quad, u):
                p = (u - 1) % 2
                quad.wait(s_lin, lambda q: QT * q + u)
                nc.vector.scalar_tensor_tensor(r0[:], p_lin, 0.0, xt[p][:], ALU.max, ALU.add).then_inc(s_r0, 1)
                quad.wait(s_r0, lambda q: QT * q + u)
                ch = Chain(dve, s_late)
                ch.then(nc.vector.bn_stats(st0[:], r0[:]))
                ch.then(nc.vector.bn_aggr(mv0[:], st0[:]))
                nc.vector.memset(r1[:], 0.0).then_inc(s_mv0, 1)
                quad.wait(s_sd0, lambda q: QT * q + u)
                ch.then(nc.vector.reciprocal(rs0[:], sd0[:]))
                ch.end()
                quad.wait(s_x1st[p], lambda q: 16 * (2 * q + (u - 1) // 2))
                quad.wait(s_x1T, lambda q: QT * q + u - 2)
                nc.vector.tensor_scalar(x1[p][:], r0[:], mv0[:, 0:1], rs0[:], ALU.subtract, ALU.mult).then_inc(s_x1, 1)

            def masked(quad, u, n):
                par = (quad.q - BQ) // BQ % 2 * JT
                jt, hh, k = QT * u + n // 2, n % 2, n % UVB
                quad.wait(s_v, lambda q: UNITS * (q - BQ) + 8 * u + n + 1)
                m = maskT[:, bass.ds((quad.q - BQ) % RING * JT + jt, 1), :].rearrange("p a i -> p (a i)")
                for i in range(2):
                    last = nc.vector.scalar_tensor_tensor(uv[k][:, i, :], uv[k][:, i, :],
                                                          dj[:, bass.ds(par + jt, 1), 2 * hh + i], m, ALU.add, ALU.mult)
                last.then_inc(s_u, 1)
                if u == QT - 1 and n == 7:
                    nc.vector.memset(r1[:], 0.0).then_inc(s_blk, 1)

            def maximum(quad, u, c):
                quad.wait(s_rows[c], lambda q: 16 * CR * (QT * q + u + 1))
                nc.vector.tensor_reduce(cmax[:, c, :], rows[:, c, :].rearrange("p (r f) -> p f r", f=C),
                                        axis=AX.X, op=ALU.max).then_inc(s_rfree, 1)

            def aggregate(quad, u):
                quad.wait(s_rfree, lambda q: CH * (QT * q + u + 2))
                quad.wait(s_xaT, lambda q: QT * q + u)
                ch = Chain(dve, s_maxc)
                ch.then(nc.vector.tensor_reduce(agg[:], cmax[:].rearrange("p c f -> p f c"), axis=AX.X, op=ALU.max))
                nc.vector.tensor_scalar(agg[:], agg[:], lim[u % 2][:, 0:1], lim[u % 2][:, 1:2], ALU.max, ALU.min).then_inc(s_agg, 1)
                ch.end()

            def norm(quad):
                quad.wait(s_pe, lambda q: UNITS * (q - BQ))
                ch = Chain(dve, s_norm)
                for i in range(QT):
                    sums = acc[i][:, 0:HEADS * HW].rearrange("p (h e) -> p h e", h=HEADS)
                    last = nc.vector.reciprocal(rden[:, i, :], sums[:, :, HO])
                ch.then(last)
                for i in range(QT):
                    sums = acc[i][:, 0:HEADS * HW].rearrange("p (h e) -> p h e", h=HEADS)
                    last = nc.vector.tensor_tensor(dst[:, i, :].rearrange("p (h e) -> p h e", h=HEADS), sums[:, :, 0:HO],
                                                   rden[:, i, :].unsqueeze(2).to_broadcast([P, HEADS, HO]), ALU.mult)
                ch.then(last)
                ch.end()
                nc.vector.memset(r1[:], 0.0).then_inc(s_accfree, 1)

            def finish(quad, u):
                p = u % 2
                m = quad.q - BQ - 1
                t = m // BQ % 2 * JT + m % BQ * QT + u
                ch = Chain(dve, s_fin)
                quad.wait(s_out, lambda q: QT * q + u - FIN)
                oh3 = oh[:].rearrange("p (h e) -> p h e", h=HEADS)

                def per_head(a):
                    return a.unsqueeze(2).to_broadcast([P, HEADS, HO])

                ch.then(nc.vector.tensor_tensor(oh[:], dst[:, u, :], bias_b[:], ALU.add))
                ch.then(nc.vector.scalar_tensor_tensor(oh3, oh3, 0.0, hs[:, bass.ds(t, 1), :, 0:HO].rearrange("p a h e -> p (a h) e"),
                                                       ALU.max, ALU.add))
                for h in range(HEADS):
                    last = nc.vector.bn_stats(sth[:, h, :], oh3[:, h, :])
                ch.then(last)
                for h in range(HEADS):
                    last = nc.vector.bn_aggr(mvh[:, h, :], sth[:, h, :])
                ch.then(last)
                nc.vector.memset(r1[:], 0.0).then_inc(s_mvh, 1)
                ch.then(nc.vector.tensor_tensor(oh3, oh3, per_head(mvh[:, :, 0]), ALU.subtract))
                quad.wait(s_sdh, lambda q: QT * q + u - FIN + 1)
                ch.then(nc.vector.reciprocal(rsh[:], sdh[:]))
                ch.then(nc.vector.tensor_tensor(oh3, oh3, per_head(rsh[:]), ALU.mult))
                ch.then(nc.vector.tensor_tensor(oh[:], oh[:], gamma_b[:], ALU.mult))
                ch.then(nc.vector.tensor_tensor(oh[:], oh[:], beta_b[:], ALU.add))
                quad.wait(s_x1r[p], lambda q: 16 * (2 * q + (u - FIN) // 2 + 1))
                ch.then(nc.vector.tensor_tensor(oh[:], oh[:], x1r[p][:], ALU.add))
                ch.then(nc.vector.bn_stats(stf[:], oh[:]))
                ch.then(nc.vector.bn_aggr(mvf[:], stf[:]))
                nc.vector.memset(r1[:], 0.0).then_inc(s_mvf, 1)
                quad.wait(s_sdf, lambda q: QT * q + u - FIN + 1)
                ch.then(nc.vector.reciprocal(rsf[:], sdf[:]))
                quad.wait(s_st[p], lambda q: 16 * (2 * q + (u - FIN) // 2))
                nc.vector.tensor_scalar(outb[p][:], oh[:], mvf[:, 0:1], rsf[:], ALU.subtract, ALU.mult).then_inc(s_out, 1)
                ch.end()

            def step(quad, u):
                if u == 0 and quad.on(u, FIN):
                    norm(quad)
                if quad.on(u, -1):
                    early(quad, u, 1)
                if quad.on(u, 1):
                    late(quad, u)
                att, gather = quad.on(u, QT * BQ), quad.on(u, 0)
                if att:
                    dve.wait_ge(s_proj, projected(quad, u))
                for n in range(8):
                    if att:
                        masked(quad, u, n)
                    if gather and n in CHUNK_AFTER:
                        maximum(quad, u, CHUNK_AFTER.index(n))
                if gather:
                    aggregate(quad, u)
                if quad.on(u, FIN):
                    finish(quad, u)

            early(Quad(dve, 0, 0, 0), 0, 0)
            run_quads(dve, step)

        @block.tensor
        def _(pe):
            pe.wait_ge(s_const, CONST)
            pe.wait_ge(s_setup, 1)

            def transpose_mask(quad, u, g_of):
                quad.wait(s_mask, lambda q: QT * q + u + g_of + 1)
                for hf in range(2):
                    quad.wait(s_ring, lambda q: 2 * (QT * q + u + g_of - 1) + hf + 1)
                    for j in range(HALF):
                        jt = hf * HALF + j
                        last = nc.tensor.transpose(pT[hf][:, j * P:(j + 1) * P], mask_sb[:, jt * P:(jt + 1) * P], id16[:])
                    last.then_inc(s_T, 1)
                quad.wait(s_stage, lambda q: 2 * (QT * q + u + g_of + 1))
                quad.wait(s_keyread, lambda q: QT * q + u + g_of)
                quad.wait(s_proj, lambda q: QT * q + u + g_of - 2)
                for jt in range(JT):
                    last = nc.tensor.matmul(p_key[:, jt * WPT:(jt + 1) * WPT], stage[:, jt, :], pack[:], start=True, stop=True)
                last.then_inc(s_key, 1)

            def spread(quad):
                for h in range(HEADS):
                    if h == 0:
                        pe.wait_ge(s_proj, projected(quad, 0))
                    else:
                        quad.wait(s_rb, lambda q: HEADS * (q - BQ) + h)
                    pe.sem_inc(s_go_pe, 1)
                    nc.tensor.matmul(pA[:, :], sel[:, h, :], esT[:, bass.ds((quad.q - BQ) % RING * IB, IB)],
                                     start=True, stop=True).then_inc(s_es, 1)

            def product0(quad, u):
                p = (u - 1) % 2
                quad.wait(s_agg, lambda q: QT * q + u)
                quad.wait(s_x[p], lambda q: 16 * (2 * q + (u - 1) // 2 + 1))
                quad.wait(s_proj, lambda q: QT * q + u - 1)
                if u == 0 and quad.on(u, QT * BQ):
                    quad.wait(s_rb, lambda q: HEADS * (q - BQ + 1))
                if quad.on(u, -1):
                    quad.wait(s_keyread, lambda q: QT * q + u + 2)
                for c in range(4):
                    src = (xt[p] if c < 2 else agg)[:, c % 2 * P:(c % 2 + 1) * P]
                    last = nc.tensor.transpose(pA[:, c * P:(c + 1) * P], src, id32[:])
                last.then_inc(s_xaT, 1)
                quad.wait(s_xaE, lambda q: QT * q + u)
                for c in range(4):
                    nc.tensor.matmul(p_lin, xaT[:, c, :], w0_sb[:, c, :], start=(c == 0), stop=False)
                nc.tensor.matmul(p_lin, ones_row[:], b0_sb[:], start=False, stop=True).then_inc(s_lin, 1)

            def product1(quad, u):
                p = (u - 1) % 2
                quad.wait(s_x1, lambda q: QT * q + u)
                for c in range(2):
                    last = nc.tensor.transpose(p_x1T[:, c * P:(c + 1) * P], x1[p][:, c * P:(c + 1) * P], id32[:])
                last.then_inc(s_x1T, 1)
                quad.wait(s_x1E, lambda q: QT * q + u)
                for c in range(2):
                    nc.tensor.matmul(p_h, x1T[:, c, :], wcat[:, c, :], start=(c == 0), stop=(c == 1))
                for c in range(2):
                    last = nc.tensor.matmul(p_es, wcat[:, c, C:C + HEADS], x1T[:, c, :], start=(c == 0), stop=(c == 1))
                last.then_inc(s_h, 1)

            def attend(quad, u, part):
                par = (quad.q - BQ) // BQ % 2 * JT
                for n in range(4 * part, 4 * part + 4):
                    jt, hh, k = QT * u + n // 2, n % 2, n % UVB
                    quad.wait(s_u, lambda q: UNITS * (q - BQ) + 8 * u + n + 1)
                    for i in range(2):
                        h = 2 * hh + i
                        for it in range(QT):
                            last = nc.tensor.matmul(acc[it][:, h * HW:(h + 1) * HW], uv[k][:, i, it * P:(it + 1) * P],
                                                    hs[:, bass.ds(par + jt, 1), h, :].rearrange("p a e -> p (a e)"),
                                                    start=(jt == 0 and h == 0), stop=(jt == JT - 1 and h == HEADS - 1),
                                                    skip_group_check=True)
                    last.then_inc(s_pe, 1)

            def step(quad, u):
                att = quad.on(u, QT * BQ)
                if quad.on(u, -1):
                    transpose_mask(quad, u, 1)
                if att and u == 0:
                    spread(quad)
                if quad.on(u, 1):
                    product0(quad, u)
                if att:
                    if u == 0:
                        quad.wait(s_accfree, lambda q: q - BQ)
                    pe.wait_ge(s_proj, projected(quad, u))
                    attend(quad, u, 0)
                    attend(quad, u, 1)
                if quad.on(u, 1):
                    product1(quad, u)

            transpose_mask(Quad(pe, 0, 0, 0), 0, 0)
            run_quads(pe, step)


def constants():
    import numpy as np
    j = np.arange(P)
    pack = np.zeros((P, WPT), np.float32)
    pack[j, j // WORD] = 2.0 ** (WORD - 1 - j % WORD)
    sel = np.zeros((HEADS, HEADS, P), np.float32)
    for h in range(HEADS):
        sel[h, h, :] = 1.0
    rows = lambda v, dt: np.tile(np.asarray(v, dt)[None, :], (P, 1))
    return {
        "id16": (np.eye(P, dtype=np.float16), F16),
        "id32": (np.eye(P, dtype=np.float32), F32),
        "pack": (pack, BF16),
        "wordkey": (rows((WORDS - 1 - np.arange(WORDS)) * 2.0 ** WORD, np.float32), F32),
        "nibkey": (rows(16.0 * (NIB - 1 - np.arange(NIB)), np.float32), F32),
        "bitmask": (rows(2 ** (NIB - 1 - np.arange(NIB)), np.int32), I32),
        "colkey": (rows(4.0 - np.arange(NIB), np.float32), F32),
        "sel": (sel, F32),
        "rowbase": (rows((np.arange(TILES) // JT + 1) * float(N), np.float32), F32),
    }


_INS = ['x', 'adj', 'L0_gnn_W', 'L0_gnn_b', 'L1_gnn_W', 'L1_gnn_a_src', 'L1_gnn_a_dst', 'L1_gnn_bias',
        'L1_gnn_ln_gamma', 'L1_gnn_ln_beta']
_OUTS = [((B, N, C), 'float32')]


def kernel(**inputs):
    import ml_dtypes
    import numpy as _np
    import concourse.bacc as _bacc
    from concourse import mybir as _mybir
    from concourse.bass_utils import run_bass_kernel_spmd as _run

    nc = _bacc.Bacc("TRN2", target_bir_lowering=False, num_devices=1)
    arrays, args = {}, []
    for name in _INS:
        a = _np.ascontiguousarray(inputs[name])
        arrays[f"in_{name}_dram"] = a
        args.append(nc.dram_tensor(f"in_{name}_dram", a.shape, _mybir.dt.from_np(a.dtype), kind="ExternalInput").ap())
    for name, (a, dt) in constants().items():
        if dt == BF16:
            a = a.astype(ml_dtypes.bfloat16)
        arrays[f"const_{name}_dram"] = a
        args.append(nc.dram_tensor(f"const_{name}_dram", a.shape, dt, kind="ExternalInput").ap())
    for i, (shape, dtype) in enumerate(_OUTS):
        dt = _mybir.dt.from_np(_np.dtype(dtype))
        args.append(nc.dram_tensor(f"out_{i}_dram", shape, dt, kind="ExternalOutput").ap())
    layers_program(nc, *args)
    r = _run(nc, [arrays], core_ids=[0])
    return r.results[0]["out_0_dram"]
```

```python
from contextlib import ExitStack

import concourse.bass as bass
from concourse import mybir

ALU = mybir.AluOpType
ACT = mybir.ActivationFunctionType
AX = mybir.AxisListType
F32 = mybir.dt.float32
F16 = mybir.dt.float16
BF16 = mybir.dt.bfloat16
I32 = mybir.dt.int32
U32 = mybir.dt.uint32
U8 = mybir.dt.uint8

P = 128
B, N, C = 8, 2048, 256
HEADS, HO = 4, 64
HW = HO + 1
S = 25
JT = N // P
TILES = B * JT
QT = 4
IB = QT * P
QUADS = TILES // QT
BQ = JT // QT
RING = 6
WORD = 16
WORDS = N // WORD
WPT = P // WORD
NIB = 4
TOP = 32
CH = 5
CR = S // CH
FIRST = S + 1
HALF = JT // 2
UNITS = JT * 2
US = UNITS // QT
UVB = 4
AHEAD = 3
BIG = 3.0e38
FIN = QT * (BQ + 1)
LN0_EPS = 1e-5
HEAD_EPS = 1e-6
LEAK = 0.01


class Quad:

    def __init__(self, eng, q, first, last):
        self.eng, self.q, self.first, self.last, self.par = eng, q, first, last, first // BQ % 2

    def on(self, u, lag):
        here = [0 <= QT * q + u - lag < TILES for q in (self.first, self.last)]
        assert here[0] == here[1]
        return here[0]

    def reach(self, count):
        if count(self.last) <= 0:
            return []
        assert count(self.first) > 0
        return [count(self.q)]


def run_quads(eng, step):
    def quad(q, first, last):
        for u in range(QT):
            step(Quad(eng, q, first, last), u)

    def loop(a, b):
        with eng.Fori(a, b) as q:
            quad(q, a, b - 1)

    quad(0, 0, 0)
    loop(1, BQ - 1)
    quad(BQ - 1, BQ - 1, BQ - 1)
    quad(BQ, BQ, BQ)
    quad(BQ + 1, BQ + 1, BQ + 1)
    loop(BQ + 2, 2 * BQ)
    with eng.Fori(1, B // 2 - 1) as pair:
        for par in range(2):
            with eng.Fori(0, BQ) as k:
                quad(pair * (2 * BQ) + (k + par * BQ), (2 + par) * BQ, (B - 4 + par + 1) * BQ - 1)
    loop(QUADS - 2 * BQ, QUADS - BQ)
    loop(QUADS - BQ, QUADS - 1)
    quad(QUADS - 1, QUADS - 1, QUADS - 1)
    quad(QUADS, QUADS, QUADS)
    loop(QUADS + 1, QUADS + BQ - 1)
    quad(QUADS + BQ - 1, QUADS + BQ - 1, QUADS + BQ - 1)
    quad(QUADS + BQ, QUADS + BQ, QUADS + BQ)
    quad(QUADS + BQ + 1, QUADS + BQ + 1, QUADS + BQ + 1)


def projected(quad, u):
    return QT * quad.q + u - 1 if QT * quad.first + u <= TILES + 1 else TILES


def after(quad, u, ahead):
    return quad.q + (u + ahead) // QT, (u + ahead) % QT


class Chain:

    def __init__(self, eng, sem, between=None):
        self.eng, self.sem, self.n, self.between = eng, sem, 0, between

    def then(self, instruction):
        self.n += 1
        instruction.then_inc(self.sem, 1)
        if self.between:
            self.between(self.n)
        self.eng.wait_ge(self.sem, self.n)

    def end(self):
        self.eng.sem_clear(self.sem)


def layers_program(nc, x, adj, w0, b0, w1, a_src, a_dst, bias1, gamma, beta,
                   c_id16, c_id32, c_pack, c_wordkey, c_nib, c_mask, c_col, c_base, out):
    x_rows = x.rearrange("b n c -> (b n) c")
    adj_rows = adj.rearrange("b n m -> (b n) m")
    out_rows = out.rearrange("b n c -> (b n) c")
    xh_dram = nc.dram_tensor("xh_dram", (B * N, 2 * C), F32).ap()
    r_dram = nc.dram_tensor("r_dram", (HEADS, B * N), F32).ap()
    xh_blocks = xh_dram.rearrange("(m i p) c -> p (m i) c", i=QT, p=P)
    out_blocks = out_rows.rearrange("(m i p) c -> p (m i) c", i=QT, p=P)

    ctx = ExitStack()
    with ctx:
        def sb(name, shape, dt):
            return ctx.enter_context(nc.sbuf_tensor(name, shape, dt))

        def ps(name, shape, dt):
            return ctx.enter_context(nc.psum_tensor(name, shape, dt))

        def sem(name):
            return ctx.enter_context(nc.semaphore(name))

        id16 = sb("id16", [P, P], F16)
        id32 = sb("id32", [P, P], F32)
        pack = sb("pack", [P, WPT], BF16)
        wordkey = sb("wordkey", [P, WORDS], F32)
        nibkey = sb("nibkey", [P, NIB], F32)
        bitmask = sb("bitmask", [P, NIB], I32)
        colkey = sb("colkey", [P, NIB], F32)
        w0_sb = sb("w0_sb", [P, 4, C], F32)
        b0_sb = sb("b0_sb", [1, C], F32)
        ones_row = sb("ones_row", [1, P], F32)
        wcat = sb("wcat", [P, 2, C + 2 * HEADS], F32)
        bias_b = sb("bias_b", [P, C], F32)
        gamma_b = sb("gamma_b", [P, C], F32)
        beta_b = sb("beta_b", [P, C], F32)
        eps0 = sb("eps0", [P, 1], F32)
        eps1 = sb("eps1", [P, 1], F32)
        rowbase = sb("rowbase", [P, TILES], F32)
        adj_sb = sb("adj_sb", [P, N], I32)
        mask_sb = sb("mask_sb", [P, N], F16)
        stage = sb("stage", [P, JT, P], BF16)
        maskT = sb("maskT", [P, RING * JT, IB], U8)
        key_a = sb("key_a", [P, WORDS], F32)
        key_b = sb("key_b", [P, WORDS], F32)
        top = sb("top", [P, TOP], F32)
        topi = sb("topi", [P, FIRST], I32)
        part = sb("part", [P, FIRST, NIB], I32)
        high = sb("high", [P, FIRST], I32)
        value = sb("value", [P, FIRST, NIB], F32)
        pad = sb("pad", [P, S], F32)
        lim = [sb(f"lim{p}", [P, 2], F32) for p in range(2)]
        idx = [sb(f"idx{p}", [P, S], U32) for p in range(2)]
        rows = sb("rows", [P, CH, CR * C], F32)
        rmax = sb("rmax", [P, CR * C], F32)
        agg = sb("agg", [P, C], F32)
        xt = [sb(f"xt{p}", [P, C], F32) for p in range(2)]
        xaT = sb("xaT", [P, 4, P], F32)
        r0 = sb("r0", [P, C], F32)
        st0 = sb("st0", [P, 6], F32)
        mv0 = sb("mv0", [P, 2], F32)
        sd0 = sb("sd0", [P, 1], F32)
        rs0 = sb("rs0", [P, 1], F32)
        xh = [sb(f"xh{p}", [P, 2, C], F32) for p in range(2)]
        x1T = sb("x1T", [P, 2, P], F32)
        hs = sb("hs", [P, 2 * JT, HEADS, HW], F32)
        qj = sb("qj", [P, 2 * JT, HEADS], F32)
        dj = sb("dj", [P, HEADS], F32)
        er = [sb(f"er{p}", [HEADS, P], F32) for p in range(2)]
        rb = sb("rb", [P, 2, HEADS, IB], F32)
        uv = [sb(f"uv{k}", [P, 2, IB], F32) for k in range(UVB)]
        sT = sb("sT", [HW, HEADS, IB], F32)
        rden = sb("rden", [P, QT, HEADS], F32)
        dst = sb("dst", [P, QT, C], F32)
        xr = sb("xr", [P, QT, C], F32)
        sth = sb("sth", [P, QT * HEADS, 6], F32)
        mvh = sb("mvh", [P, QT * HEADS, 2], F32)
        sdh = sb("sdh", [P, QT * HEADS], F32)
        rsh = sb("rsh", [P, QT * HEADS], F32)
        stf = sb("stf", [P, QT, 6], F32)
        mvf = sb("mvf", [P, QT, 2], F32)
        sdf = sb("sdf", [P, QT], F32)
        rsf = sb("rsf", [P, QT], F32)
        tick = sb("tick", [P, 6], F32)

        acc = [ps(f"acc{i}", [P, 512], F32) for i in range(QT)]
        pT = [ps(f"pT{i}", [P, HALF * P], F16) for i in range(2)]
        pA = ps("pA", [P, 512], F32)
        pB = ps("pB", [P, 512], F32)
        p_lin, p_key = pB[:, 0:C], pB[:, 384:384 + WORDS]
        p_h = pB[:, 0:C + 2 * HEADS]
        p_ed = pB[:, C + HEADS:C + 2 * HEADS]
        p_x1T, p_es = pA[:, 0:2 * P], pA[0:HEADS, 2 * P:3 * P]

        s_const = sem("s_const")
        s_go = {e: sem(f"s_go_{e}") for e in ("sp", "act", "pool")}
        s_setup = sem("s_setup")
        s_wa = sem("s_wa")
        s_adj = sem("s_adj")
        s_x = [sem(f"s_xin{p}") for p in range(2)]
        s_mask = sem("s_mask")
        s_T = sem("s_T")
        s_stage = sem("s_stage")
        s_ring = sem("s_ring")
        s_key = sem("s_key")
        s_keyread = sem("s_keyread")
        s_topk = sem("s_topk")
        s_idx = sem("s_idx")
        s_rows = [sem(f"s_rows{c}") for c in range(CH)]
        s_rfree = sem("s_rfree")
        s_maxc = sem("s_maxc")
        s_agg = sem("s_agg")
        s_xaT = sem("s_xaT")
        s_xaE = sem("s_xaE")
        s_lin = sem("s_lin")
        s_r0 = sem("s_r0")
        s_late = sem("s_late")
        s_mv0 = sem("s_mv0")
        s_sd0 = sem("s_sd0")
        s_x1 = sem("s_x1")
        s_xhst = [sem(f"s_xhst{p}") for p in range(2)]
        s_rst = [sem(f"s_rst{p}") for p in range(2)]
        s_x1T = sem("s_x1T")
        s_x1E = sem("s_x1E")
        s_h = sem("s_h")
        s_proj = sem("s_proj")
        s_ed = sem("s_ed")
        s_rb = sem("s_rb")
        s_v = sem("s_v")
        s_u = sem("s_u")
        s_pe = sem("s_pe")
        s_blk = sem("s_blk")
        s_sT = sem("s_sT")
        s_back = sem("s_back")
        s_accfree = sem("s_accfree")
        s_norm = sem("s_norm")
        s_hload = sem("s_hload")
        s_hused = sem("s_hused")
        s_x1load = sem("s_x1load")
        s_fin = sem("s_fin")
        s_mvh = sem("s_mvh")
        s_sdh = sem("s_sdh")
        s_mvf = sem("s_mvf")
        s_sdf = sem("s_sdf")
        s_out = sem("s_out")
        s_st = sem("s_st")

        consts = [(id16[:], c_id16), (id32[:], c_id32), (pack[:], c_pack), (wordkey[:], c_wordkey),
                  (nibkey[:], c_nib), (bitmask[:], c_mask), (colkey[:], c_col),
                  (w0_sb[:], w0.rearrange("(c p) o -> p c o", p=P)),
                  (b0_sb[:], b0.rearrange("(a n) -> a n", a=1)),
                  (bias_b[:], bias1.rearrange("h e -> (h e)").partition_broadcast(P)),
                  (gamma_b[:], gamma.rearrange("h e -> (h e)").partition_broadcast(P)),
                  (beta_b[:], beta.rearrange("h e -> (h e)").partition_broadcast(P)),
                  (rowbase[:], c_base),
                  (dst[:, 0, :].rearrange("p (h e) -> p h e", h=HEADS), a_src[:, 0, :].partition_broadcast(P)),
                  (dst[:, 1, :].rearrange("p (h e) -> p h e", h=HEADS), a_dst[:, 0, :].partition_broadcast(P)),
                  (wcat[:, 0, 0:C].rearrange("p (h e) -> p h e", h=HEADS), w1.rearrange("h (c p) e -> p c h e", p=P)[:, 0]),
                  (wcat[:, 1, 0:C].rearrange("p (h e) -> p h e", h=HEADS), w1.rearrange("h (c p) e -> p c h e", p=P)[:, 1])]
        CONST = 16 * len(consts)


        block = ctx.enter_context(nc.Block())

        @block.sync
        def _(sp):
            for dst_ap, src in consts:
                sp.dma_start(dst_ap, src).then_inc(s_const, 16)
            sp.dma_start(adj_sb[:], adj_rows[0:P, :]).then_inc(s_adj, 16)
            sp.wait_ge(s_mask, 1)
            sp.dma_start(adj_sb[:], adj_rows[P:2 * P, :]).then_inc(s_adj, 16)

            def step(quad, u):
                s, p = QT * quad.q + u, u % 2
                if quad.on(u, -2):
                    for v in quad.reach(lambda q: QT * q + u + 2):
                        sp.wait_ge(s_mask, v)
                        sp.sem_inc(s_go["sp"], 1)
                    sp.dma_start(adj_sb[:], adj_rows[bass.ds((s + 2) * P, P), :]).then_inc(s_adj, 16)
                if quad.on(u, 0):
                    for v in quad.reach(lambda q: QT * q + u - 1):
                        sp.wait_ge(s_r0, v)
                        sp.sem_inc(s_go["sp"], 1)
                    sp.dma_start(xt[p][:], x_rows[bass.ds(s * P, P), :]).then_inc(s_x[p], 16)
                if quad.on(u, 2):
                    for v in quad.reach(lambda q: QT * q + u - 1):
                        sp.wait_ge(s_proj, v)
                        sp.sem_inc(s_go["sp"], 1)
                    sp.dma_start(xh_dram[bass.ds((s - 2) * P, P), :], xh[p][:].rearrange("p a c -> p (a c)")).then_inc(s_xhst[p], 16)
                    sp.dma_start(r_dram[:, bass.ds((s - 2) * P, P)], er[p][:]).then_inc(s_rst[p], 16)
                if u == 1 and quad.on(u, QT * BQ - QT):
                    m = quad.q - BQ + 1
                    for o in range(2):
                        for v in quad.reach(lambda q: 32 * (q - BQ + 2)):
                            sp.wait_ge(s_rst[o], v)
                            sp.sem_inc(s_go["sp"], 1)
                    for v in quad.reach(lambda q: UNITS * (q - BQ)):
                        sp.wait_ge(s_v, v)
                        sp.sem_inc(s_go["sp"], 1)
                    dst_rb = rb[:, bass.ds(m % 2, 1), :, :].rearrange("p a h i -> p (a h) i")
                    src_rb = r_dram[:, bass.ds(m * IB, IB)].partition_broadcast(P)
                    sp.dma_start(dst_rb, src_rb).then_inc(s_rb, 16)
                fin = quad.on(u, FIN)
                if u == 0 and quad.on(u, FIN + QT):
                    for v in quad.reach(lambda q: q - BQ - 1):
                        sp.wait_ge(s_out, v)
                        sp.sem_inc(s_go["sp"], 1)
                    sp.dma_start(out_blocks[:, bass.ds((quad.q - BQ - 2) * QT, QT), :], xr[:]).then_inc(s_st, 16)
                if fin and u == 0:
                    for v in quad.reach(lambda q: 16 * (q - BQ - 1)):
                        sp.wait_ge(s_st, v)
                        sp.sem_inc(s_go["sp"], 1)
                    for o in range(2):
                        for v in quad.reach(lambda q: 32 * (q - BQ)):
                            sp.wait_ge(s_xhst[o], v)
                            sp.sem_inc(s_go["sp"], 1)
                    sp.dma_start(xr[:], xh_blocks[:, bass.ds((quad.q - BQ - 1) * QT, QT), C:2 * C]).then_inc(s_hload, 16)
                if fin and u == 2:
                    for v in quad.reach(lambda q: q - BQ):
                        sp.wait_ge(s_hused, v)
                        sp.sem_inc(s_go["sp"], 1)
                    sp.dma_start(xr[:], xh_blocks[:, bass.ds((quad.q - BQ - 1) * QT, QT), 0:C]).then_inc(s_x1load, 16)

            run_quads(sp, step)
            sp.wait_ge(s_st, 16 * QUADS)
            for p in range(2):
                sp.wait_ge(s_xhst[p], 16 * TILES // 2)
                sp.wait_ge(s_rst[p], 16 * TILES // 2)

        @block.gpsimd
        def _(pool):
            def step(quad, u):
                if not quad.on(u, 0):
                    return
                p = u % 2
                for v in quad.reach(lambda q: QT * q + u + 1):
                    pool.wait_ge(s_idx, v)
                for c in range(CH):
                    for v in quad.reach(lambda q: CH * (QT * q + u) + c + 1):
                        pool.wait_ge(s_rfree, v)
                        pool.sem_inc(s_go["pool"], 1)
                    for r in range(CR):
                        k = c * CR + r
                        nc.gpsimd.indirect_dma_start(
                            rows[:, c, r * C:(r + 1) * C], None, x_rows,
                            bass.IndirectOffsetOnAxis(ap=idx[p][:, k:k + 1], axis=0)).then_inc(s_rows[c], 16)

            run_quads(pool, step)

        @block.scalar
        def _(act):
            act.wait_ge(s_const, CONST)
            act.wait_ge(s_setup, 1)

            def mask(quad, u, g_of):
                for v in quad.reach(lambda q: 16 * (QT * q + u + g_of + 1)):
                    act.wait_ge(s_adj, v)
                for v in quad.reach(lambda q: 2 * (QT * q + u + g_of)):
                    act.wait_ge(s_T, v)
                nc.scalar.activation(mask_sb[:], adj_sb[:], ACT.Sign).then_inc(s_mask, 1)

            def transposed(quad, u, g_of):
                qg, ug = after(quad, u, g_of)
                for hf in range(2):
                    for v in quad.reach(lambda q: 2 * (QT * q + u + g_of) + hf + 1):
                        act.wait_ge(s_T, v)
                    for v in quad.reach(lambda q: QT * q + u + g_of):
                        act.wait_ge(s_key, v)
                    src = pT[hf][:, :].rearrange("p (j i) -> p j i", i=P)
                    nc.scalar.activation(stage[:, hf * HALF:(hf + 1) * HALF, :], src, ACT.Square).then_inc(s_stage, 1)
                    for v in quad.reach(lambda q: q + (u + g_of) // QT + 1):
                        act.wait_ge(s_blk, v)
                    nc.scalar.activation(maskT[:, bass.ds(qg % RING * JT + hf * HALF, HALF), ug * P:(ug + 1) * P],
                                         src, ACT.Square).then_inc(s_ring, 1)

            def scaled(quad, u, n, ahead=0):
                ua = (u + ahead) % QT
                jt, hh, k = QT * ua + n // 2, n % 2, n % UVB
                qa = quad.q + (u + ahead) // QT
                if u + ahead < QT:
                    q_j = lambda h: qj[:, (1 - quad.par) * JT + jt, h:h + 1]
                else:
                    slot = (qa - BQ) // BQ % 2 * JT + jt
                    q_j = lambda h: qj[:, bass.ds(slot, 1), h:h + 1].rearrange("p a h -> p (a h)")
                for v in quad.reach(lambda q: UNITS * (q - BQ) + US * (u + ahead) + n - UVB + 1):
                    act.wait_ge(s_pe, v)
                    act.sem_inc(s_go["act"], 1)
                for i in range(2):
                    h = 2 * hh + i
                    last = nc.scalar.activation(uv[k][:, i, :], rb[:, bass.ds(qa % 2, 1), h, :].rearrange("p a i -> p (a i)"),
                                                ACT.Copy, scale=q_j(h))
                last.then_inc(s_v, 1)

            def scaled_units(quad, u, a, b):
                if quad.on(u, QT * BQ):
                    for n in range(a, b):
                        scaled(quad, u, n)

            def step(quad, u):
                next_attends = quad.on(u, QT * BQ - 1)
                if quad.on(u, QT * BQ) or next_attends:
                    act.wait_ge(s_proj, projected(quad, u))
                if quad.on(u, 1):
                    for v in quad.reach(lambda q: QT * q + u):
                        act.wait_ge(s_xaT, v)
                    for v in quad.reach(lambda q: QT * q + u - 1):
                        act.wait_ge(s_lin, v)
                    nc.scalar.activation(xaT[:, :, :], pA[:, :].rearrange("p (c i) -> p c i", c=4), ACT.Copy).then_inc(s_xaE, 1)
                if u == 0 and quad.on(u, FIN):
                    for v in quad.reach(lambda q: UNITS * (q - BQ)):
                        act.wait_ge(s_pe, v)
                    for v in quad.reach(lambda q: q - BQ - 1):
                        act.wait_ge(s_back, v)
                    for h in range(HEADS):
                        last = nc.scalar.activation(sT[:, h, :], acc[h][0:HW, :], ACT.Copy)
                    last.then_inc(s_sT, 1)
                scaled_units(quad, u, AHEAD, 4)
                if quad.on(u, -2):
                    mask(quad, u, 2)
                if quad.on(u, 1):
                    for v in quad.reach(lambda q: QT * q + u):
                        act.wait_ge(s_mv0, v)
                    nc.scalar.activation(sd0[:], mv0[:, 1:2], ACT.Sqrt, bias=eps0[:]).then_inc(s_sd0, 1)
                if u == 2 and quad.on(u, FIN):
                    for v in quad.reach(lambda q: q - BQ):
                        act.wait_ge(s_mvh, v)
                    nc.scalar.activation(sdh[:], mvh[:, :, 1], ACT.Sqrt, bias=eps1[:]).then_inc(s_sdh, 1)
                scaled_units(quad, u, 4, 6)
                if quad.on(u, 1):
                    project(quad, u)
                scaled_units(quad, u, 6, 7)
                if quad.on(u, -2):
                    transposed(quad, u, 2)
                scaled_units(quad, u, 7, 8)
                if u == 3 and quad.on(u, FIN):
                    for v in quad.reach(lambda q: q - BQ):
                        act.wait_ge(s_mvf, v)
                    nc.scalar.activation(sdf[:], mvf[:, :, 1], ACT.Sqrt, bias=eps0[:]).then_inc(s_sdf, 1)
                if next_attends:
                    if u == QT - 1:
                        for v in quad.reach(lambda q: 16 * (q - BQ + 2)):
                            act.wait_ge(s_rb, v)
                            act.sem_inc(s_go["act"], 1)
                    for n in range(AHEAD):
                        scaled(quad, u, n, 1)

            def project(quad, u):
                p = (u - 1) % 2
                qg, ug = after(quad, u, -1)
                for v in quad.reach(lambda q: QT * q + u):
                    act.wait_ge(s_x1T, v)
                nc.scalar.activation(x1T[:, :, :], p_x1T.rearrange("p (c i) -> p c i", c=2), ACT.Copy).then_inc(s_x1E, 1)
                for v in quad.reach(lambda q: QT * q + u):
                    act.wait_ge(s_h, v)
                for v in quad.reach(lambda q: UNITS * (q + (u - 1) // QT - BQ)):
                    act.wait_ge(s_pe, v)
                for v in quad.reach(lambda q: 16 * (2 * q + (u - 1) // 2)):
                    act.wait_ge(s_rst[p], v)
                t = qg // BQ % 2 * JT + qg % BQ * QT + ug
                nc.scalar.activation(dj[:], p_ed, ACT.Exp, scale=LEAK).then_inc(s_ed, 1)
                nc.scalar.activation(qj[:, bass.ds(t, 1), :], p_ed.unsqueeze(1), ACT.Exp, scale=1.0 - LEAK)
                nc.scalar.activation(er[p][:], p_es, ACT.Exp, scale=1.0 - LEAK)
                nc.scalar.activation(xh[p][:, 1, :], pB[:, 0:C], ACT.Copy)
                for v in quad.reach(lambda q: QT * q + u):
                    act.wait_ge(s_ed, v)
                nc.scalar.activation(hs[:, bass.ds(t, 1), :, HO], dj[:].unsqueeze(1), ACT.Copy)
                for h in range(HEADS):
                    last = nc.scalar.activation(hs[:, bass.ds(t, 1), h, 0:HO], pB[:, h * HO:(h + 1) * HO].unsqueeze(1), ACT.Copy,
                                                scale=dj[:, h:h + 1])
                last.then_inc(s_proj, 1)

            for g in range(2):
                mask(Quad(act, 0, 0, 0), 0, g)
                transposed(Quad(act, 0, 0, 0), 0, g)
            run_quads(act, step)

        @block.vector
        def _(dve):
            nc.vector.memset(ones_row[:], 1.0)
            nc.vector.memset(eps0[:], LN0_EPS)
            nc.vector.memset(eps1[:], HEAD_EPS).then_inc(s_rfree, CH)
            dve.wait_ge(s_const, CONST)
            for c in range(2):
                for k in range(2):
                    nc.vector.tensor_tensor(r0[:], wcat[:, c, 0:C], dst[:, k, :], ALU.mult).then_inc(s_wa, 1)
                    dve.wait_ge(s_wa, 4 * c + 2 * k + 1)
                    nc.vector.tensor_reduce(wcat[:, c, C + HEADS * k:C + HEADS * (k + 1)],
                                            r0[:].rearrange("p (h e) -> p h e", h=HEADS), axis=AX.X, op=ALU.add).then_inc(s_wa, 1)
                    dve.wait_ge(s_wa, 4 * c + 2 * k + 2)
            nc.vector.memset(r0[:, 0:1], 0.0).then_inc(s_blk, RING)
            nc.vector.memset(r0[:, 1:2], 0.0).then_inc(s_setup, 1)

            def top32(ch, keys):
                a, b = key_a[:, 0:keys], key_b[:, 0:keys]
                for k in range(0, TOP, 8):
                    ch.then(nc.vector.max(top[:, k:k + 8], a))
                    if k + 8 < TOP:
                        ch.then(nc.vector.match_replace(b, top[:, k:k + 8], a, 0.0))
                        a, b = b, a

            a3, b3 = (k[:, 0:FIRST * NIB].rearrange("p (t n) -> p t n", n=NIB) for k in (key_a, key_b))

            def search_words(quad, u, g_of, ch):
                for v in quad.reach(lambda q: QT * q + u + g_of + 1):
                    dve.wait_ge(s_key, v)
                ch.then(nc.vector.scalar_tensor_tensor(key_b[:], p_key, 0.0, wordkey[:], ALU.is_gt, ALU.mult))
                ch.then(nc.vector.tensor_tensor(key_a[:], p_key, key_b[:], ALU.add))
                nc.vector.memset(pad[:, 0:1], 0.0).then_inc(s_keyread, 1)
                top32(ch, WORDS)

            def search_nibbles(ch):
                ch.then(nc.vector.tensor_copy(topi[:], top[:, 0:FIRST]))
                nc.vector.tensor_scalar(high[:], topi[:], 10, (WORDS - 1) << 6, ALU.logical_shift_right, ALU.bitwise_and)
                for n in range(NIB):
                    last = nc.vector.tensor_scalar(part[:, :, n], topi[:], WORD - NIB * (n + 1), 15,
                                                   ALU.logical_shift_right, ALU.bitwise_and)
                ch.then(last)
                ch.then(nc.vector.tensor_tensor(value[:], high[:].unsqueeze(2).to_broadcast([P, FIRST, NIB]),
                                                nibkey[:].unsqueeze(1).to_broadcast([P, FIRST, NIB]), ALU.add))
                ch.then(nc.vector.scalar_tensor_tensor(b3, part[:], 0.0, value[:], ALU.is_gt, ALU.mult))
                ch.then(nc.vector.tensor_tensor(a3, part[:], b3, ALU.add))
                top32(ch, FIRST * NIB)

            def search_columns(quad, u, g_of, ch):
                p = (u + g_of) % 2
                g = QT * quad.q + u + g_of
                ch.then(nc.vector.tensor_copy(topi[:], top[:, 0:FIRST]))
                nc.vector.tensor_scalar(high[:], topi[:], 2, N - NIB, ALU.logical_shift_right, ALU.bitwise_and)
                ch.then(nc.vector.tensor_tensor(part[:], topi[:].unsqueeze(2).to_broadcast([P, FIRST, NIB]),
                                                bitmask[:].unsqueeze(1).to_broadcast([P, FIRST, NIB]), ALU.bitwise_and))
                ch.then(nc.vector.tensor_tensor(value[:], high[:].unsqueeze(2).to_broadcast([P, FIRST, NIB]),
                                                colkey[:].unsqueeze(1).to_broadcast([P, FIRST, NIB]), ALU.add))
                ch.then(nc.vector.scalar_tensor_tensor(a3, part[:], 0.0, value[:], ALU.is_gt, ALU.mult))
                top32(ch, FIRST * NIB)
                nc.vector.tensor_scalar(lim[p][:, 0:1], top[:, S:S + 1], 0.0, -BIG, ALU.is_gt, ALU.mult)
                nc.vector.tensor_scalar(lim[p][:, 1:2], top[:, 0:1], 0.0, BIG, ALU.is_gt, ALU.mult)
                ch.then(nc.vector.tensor_scalar(pad[:], top[:, 0:S], 0.0, top[:, 0:1], ALU.is_equal, ALU.mult))
                ch.then(nc.vector.tensor_tensor(pad[:], pad[:], top[:, 0:S], ALU.add))
                ch.then(nc.vector.tensor_scalar(pad[:], pad[:], 1.0, -1.0, ALU.max, ALU.mult))
                nc.vector.tensor_scalar(idx[p][:], pad[:], rowbase[:, bass.ds(g, 1)], None, ALU.add).then_inc(s_idx, 1)
                ch.end()

            def residual(quad, u, part):
                p = (u - 1) % 2
                if part == 0:
                    for v in quad.reach(lambda q: QT * q + u):
                        dve.wait_ge(s_lin, v)
                    nc.vector.scalar_tensor_tensor(r0[:], p_lin, 0.0, xt[p][:], ALU.max, ALU.add).then_inc(s_r0, 1)
                if part == 1:
                    for v in quad.reach(lambda q: QT * q + u):
                        dve.wait_ge(s_r0, v)
                    nc.vector.bn_stats(st0[:], r0[:]).then_inc(s_late, 1)
                if part == 2:
                    dve.wait_ge(s_late, 1)
                    nc.vector.bn_aggr(mv0[:], st0[:]).then_inc(s_late, 1)
                if part == 3:
                    dve.wait_ge(s_late, 2)
                    nc.vector.memset(tick[:, 5:6], 0.0).then_inc(s_mv0, 1)

            def norm0(quad, u, part):
                p = (u - 1) % 2
                if part == 0:
                    for v in quad.reach(lambda q: QT * q + u):
                        dve.wait_ge(s_sd0, v)
                    nc.vector.reciprocal(rs0[:], sd0[:]).then_inc(s_late, 1)
                if part == 1:
                    dve.wait_ge(s_late, 3)
                    dve.sem_clear(s_late)
                    for v in quad.reach(lambda q: 16 * (2 * q + (u - 1) // 2)):
                        dve.wait_ge(s_xhst[p], v)
                    for v in quad.reach(lambda q: QT * q + u - 2):
                        dve.wait_ge(s_x1T, v)
                    nc.vector.tensor_scalar(xh[p][:, 0, :], r0[:], mv0[:, 0:1], rs0[:], ALU.subtract, ALU.mult).then_inc(s_x1, 1)

            def masked(quad, u, n):
                jt, k = QT * u + n // 2, n % UVB
                for v in quad.reach(lambda q: UNITS * (q - BQ) + US * u + n + 1):
                    dve.wait_ge(s_v, v)
                m = maskT[:, bass.ds((quad.q - BQ) % RING * JT + jt, 1), :].to_broadcast([P, 2, IB])
                nc.vector.scalar_tensor_tensor(uv[k][:], uv[k][:], 1.0, m, ALU.max, ALU.mult).then_inc(s_u, 1)
                if u == QT - 1 and n == US - 1:
                    nc.vector.memset(tick[:, 4:5], 0.0).then_inc(s_blk, 1)

            def maximum(quad, u, c):
                if c == 1:
                    for v in quad.reach(lambda q: 16 * CR * (QT * q + u + 1)):
                        dve.wait_ge(s_rows[0], v)
                else:
                    for v in quad.reach(lambda q: CH * (QT * q + u + 1) + c):
                        dve.wait_ge(s_rfree, v)
                for v in quad.reach(lambda q: 16 * CR * (QT * q + u + 1)):
                    dve.wait_ge(s_rows[c], v)
                before = rows[:, 0, :] if c == 1 else rmax[:]
                nc.vector.tensor_tensor(rmax[:], before, rows[:, c, :], ALU.max).then_inc(s_rfree, 2 if c == 1 else 1)

            def aggregate(quad, u):
                for v in quad.reach(lambda q: CH * (QT * q + u + 2)):
                    dve.wait_ge(s_rfree, v)
                for v in quad.reach(lambda q: QT * q + u):
                    dve.wait_ge(s_xaT, v)
                ch = Chain(dve, s_maxc)
                ch.then(nc.vector.tensor_reduce(agg[:], rmax[:].rearrange("p (r f) -> p f r", f=C), axis=AX.X, op=ALU.max))
                nc.vector.tensor_scalar(agg[:], agg[:], lim[u % 2][:, 0:1], lim[u % 2][:, 1:2], ALU.max, ALU.min).then_inc(s_agg, 1)
                ch.end()

            def divide(quad):
                for v in quad.reach(lambda q: q - BQ):
                    dve.wait_ge(s_back, v)
                for v in quad.reach(lambda q: q - BQ - 1):
                    dve.wait_ge(s_out, v)
                ch = Chain(dve, s_norm)
                sums = [a[:, 0:HEADS * HW].rearrange("p (h e) -> p h e", h=HEADS) for a in acc]
                for i in range(QT):
                    last = nc.vector.reciprocal(rden[:, i, :], sums[i][:, :, HO])
                ch.then(last)
                for i in range(QT):
                    last = nc.vector.tensor_tensor(dst[:, i, :].rearrange("p (h e) -> p h e", h=HEADS), sums[i][:, :, 0:HO],
                                                   rden[:, i, :].unsqueeze(2).to_broadcast([P, HEADS, HO]), ALU.mult)
                ch.then(last)
                ch.end()
                nc.vector.memset(tick[:, 3:4], 0.0).then_inc(s_accfree, 1)

            heads = dst[:].rearrange("p i (h e) -> p (i h) e", h=HEADS)

            def per_head(a):
                return a.unsqueeze(2).to_broadcast([P, QT * HEADS, HO])

            def per_column(a):
                return a[:].unsqueeze(1).to_broadcast([P, QT, C])

            def finish_heads(quad, part):
                if part == 0:
                    nc.vector.tensor_tensor(dst[:], dst[:], per_column(bias_b), ALU.add).then_inc(s_fin, 1)
                if part == 1:
                    dve.wait_ge(s_fin, 1)
                    for v in quad.reach(lambda q: 16 * (q - BQ)):
                        dve.wait_ge(s_hload, v)
                    nc.vector.scalar_tensor_tensor(dst[:], dst[:], 0.0, xr[:], ALU.max, ALU.add).then_inc(s_fin, 1)
                if part == 2:
                    dve.wait_ge(s_fin, 2)
                    nc.vector.memset(tick[:, 0:1], 0.0).then_inc(s_hused, 1)
                    for h in range(QT * HEADS):
                        last = nc.vector.bn_stats(sth[:, h, :], heads[:, h, :])
                    last.then_inc(s_fin, 1)
                if part == 3:
                    dve.wait_ge(s_fin, 3)
                    for h in range(QT * HEADS):
                        last = nc.vector.bn_aggr(mvh[:, h, :], sth[:, h, :])
                    last.then_inc(s_fin, 1)
                if part == 4:
                    dve.wait_ge(s_fin, 4)
                    dve.sem_clear(s_fin)
                    nc.vector.memset(tick[:, 1:2], 0.0).then_inc(s_mvh, 1)

            def finish_norm(quad, part):
                if part == 0:
                    nc.vector.tensor_tensor(heads, heads, per_head(mvh[:, :, 0]), ALU.subtract).then_inc(s_fin, 1)
                if part == 1:
                    for v in quad.reach(lambda q: q - BQ):
                        dve.wait_ge(s_sdh, v)
                    nc.vector.reciprocal(rsh[:], sdh[:]).then_inc(s_fin, 1)
                if part == 2:
                    dve.wait_ge(s_fin, 2)
                    nc.vector.tensor_tensor(heads, heads, per_head(rsh[:]), ALU.mult).then_inc(s_fin, 1)
                if part == 3:
                    dve.wait_ge(s_fin, 3)
                    nc.vector.tensor_tensor(dst[:], dst[:], per_column(gamma_b), ALU.mult).then_inc(s_fin, 1)
                if part == 4:
                    dve.wait_ge(s_fin, 4)
                    nc.vector.tensor_tensor(dst[:], dst[:], per_column(beta_b), ALU.add).then_inc(s_fin, 1)
                if part == 5:
                    dve.wait_ge(s_fin, 5)
                    dve.sem_clear(s_fin)

            def finish_sums(quad, part):
                if part == 0:
                    for v in quad.reach(lambda q: 16 * (q - BQ)):
                        dve.wait_ge(s_x1load, v)
                    nc.vector.tensor_tensor(dst[:], dst[:], xr[:], ALU.add).then_inc(s_fin, 1)
                if part == 1:
                    dve.wait_ge(s_fin, 1)
                    for i in range(QT):
                        last = nc.vector.bn_stats(stf[:, i, :], dst[:, i, :])
                    last.then_inc(s_fin, 1)
                if part == 2:
                    dve.wait_ge(s_fin, 2)
                    for i in range(QT):
                        last = nc.vector.bn_aggr(mvf[:, i, :], stf[:, i, :])
                    last.then_inc(s_fin, 1)
                if part == 3:
                    dve.wait_ge(s_fin, 3)
                    dve.sem_clear(s_fin)
                    nc.vector.memset(tick[:, 2:3], 0.0).then_inc(s_mvf, 1)

            def finish_rows(quad):
                ch = Chain(dve, s_fin)
                for v in quad.reach(lambda q: q - BQ):
                    dve.wait_ge(s_sdf, v)
                ch.then(nc.vector.reciprocal(rsf[:], sdf[:]))
                for i in range(QT):
                    last = nc.vector.tensor_scalar(xr[:, i, :], dst[:, i, :], mvf[:, i, 0:1], rsf[:, i:i + 1], ALU.subtract, ALU.mult)
                last.then_inc(s_out, 1)
                ch.end()

            LINKS = 35
            UNIT_AT = (2, 4, 6, 14, 21, 30)
            CHUNK_AT = (13, 19, 26)
            RESIDUAL_AT = (7, 8, 9, 10)
            DIVIDE_AT = 11
            NORM_AT = (15, 16)
            FINISH_AT = (18, 20, 23, 24, 25, 28)

            def step(quad, u):
                ahead, behind, att, gather, fin = (quad.on(u, lag) for lag in (-1, 1, QT * BQ, 0, FIN))

                def between(place):
                    if att and place in UNIT_AT:
                        masked(quad, u, 1 + UNIT_AT.index(place))
                    if behind and place in RESIDUAL_AT:
                        residual(quad, u, RESIDUAL_AT.index(place))
                    if fin and u == 0 and place == DIVIDE_AT:
                        divide(quad)
                    if behind and place in NORM_AT:
                        norm0(quad, u, NORM_AT.index(place))
                    if gather and place in CHUNK_AT:
                        maximum(quad, u, 1 + CHUNK_AT.index(place))
                    if fin and place in FINISH_AT and u > 0:
                        (finish_heads, finish_norm, finish_sums)[u - 1](quad, FINISH_AT.index(place))

                if att:
                    masked(quad, u, 0)
                if ahead:
                    search = Chain(dve, s_topk, between)
                    search_words(quad, u, 1, search)
                    search_nibbles(search)
                    search_columns(quad, u, 1, search)
                    assert search.n == LINKS
                else:
                    for place in range(1, LINKS + 1):
                        between(place)
                if gather:
                    maximum(quad, u, CH - 1)
                    aggregate(quad, u)
                if att:
                    masked(quad, u, US - 1)
                if fin and u == QT - 1:
                    finish_rows(quad)

            search = Chain(dve, s_topk)
            search_words(Quad(dve, 0, 0, 0), 0, 0, search)
            search_nibbles(search)
            search_columns(Quad(dve, 0, 0, 0), 0, 0, search)
            run_quads(dve, step)

        @block.tensor
        def _(pe):
            pe.wait_ge(s_const, CONST)
            pe.wait_ge(s_setup, 1)

            def transpose_mask(quad, u, g_of):
                for v in quad.reach(lambda q: QT * q + u + g_of + 1):
                    pe.wait_ge(s_mask, v)
                for hf in range(2):
                    for v in quad.reach(lambda q: 2 * (QT * q + u + g_of - 1) + hf + 1):
                        pe.wait_ge(s_ring, v)
                    for j in range(HALF):
                        jt = hf * HALF + j
                        last = nc.tensor.transpose(pT[hf][:, j * P:(j + 1) * P], mask_sb[:, jt * P:(jt + 1) * P], id16[:])
                    last.then_inc(s_T, 1)

            def pack_words(quad, u, g_of):
                for v in quad.reach(lambda q: 2 * (QT * q + u + g_of + 1)):
                    pe.wait_ge(s_stage, v)
                for v in quad.reach(lambda q: QT * q + u + g_of):
                    pe.wait_ge(s_keyread, v)
                for v in quad.reach(lambda q: QT * q + u + g_of - 2):
                    pe.wait_ge(s_proj, v)
                for jt in range(JT):
                    last = nc.tensor.matmul(p_key[:, jt * WPT:(jt + 1) * WPT], stage[:, jt, :], pack[:], start=True, stop=True)
                last.then_inc(s_key, 1)

            def back(quad):
                for v in quad.reach(lambda q: q - BQ):
                    pe.wait_ge(s_sT, v)
                for i in range(QT):
                    for h in range(HEADS):
                        last = nc.tensor.transpose(acc[i][:, h * HW:(h + 1) * HW], sT[:, h, i * P:(i + 1) * P], id32[0:HW, 0:HW])
                last.then_inc(s_back, 1)

            def product0(quad, u):
                p = (u - 1) % 2
                for v in quad.reach(lambda q: QT * q + u):
                    pe.wait_ge(s_agg, v)
                for v in quad.reach(lambda q: 16 * (2 * q + (u - 1) // 2 + 1)):
                    pe.wait_ge(s_x[p], v)
                for v in quad.reach(lambda q: QT * q + u - 1):
                    pe.wait_ge(s_proj, v)
                if quad.on(u, -1):
                    for v in quad.reach(lambda q: QT * q + u + 2):
                        pe.wait_ge(s_keyread, v)
                for c in range(4):
                    src = (xt[p] if c < 2 else agg)[:, c % 2 * P:(c % 2 + 1) * P]
                    last = nc.tensor.transpose(pA[:, c * P:(c + 1) * P], src, id32[:])
                last.then_inc(s_xaT, 1)
                for v in quad.reach(lambda q: QT * q + u):
                    pe.wait_ge(s_xaE, v)
                for c in range(4):
                    nc.tensor.matmul(p_lin, xaT[:, c, :], w0_sb[:, c, :], start=(c == 0), stop=False)
                nc.tensor.matmul(p_lin, ones_row[:], b0_sb[:], start=False, stop=True).then_inc(s_lin, 1)

            def product1(quad, u):
                p = (u - 1) % 2
                for v in quad.reach(lambda q: QT * q + u):
                    pe.wait_ge(s_x1, v)
                for c in range(2):
                    last = nc.tensor.transpose(p_x1T[:, c * P:(c + 1) * P], xh[p][:, 0, c * P:(c + 1) * P], id32[:])
                last.then_inc(s_x1T, 1)
                for v in quad.reach(lambda q: QT * q + u):
                    pe.wait_ge(s_x1E, v)
                for c in range(2):
                    nc.tensor.matmul(p_h, x1T[:, c, :], wcat[:, c, :], start=(c == 0), stop=(c == 1))
                for c in range(2):
                    last = nc.tensor.matmul(p_es, wcat[:, c, C:C + HEADS], x1T[:, c, :], start=(c == 0), stop=(c == 1))
                last.then_inc(s_h, 1)

            def attend(quad, u, a, b):
                if not quad.on(u, QT * BQ):
                    return
                for n in range(a, b):
                    jt, hh, k = QT * u + n // 2, n % 2, n % UVB
                    for v in quad.reach(lambda q: UNITS * (q - BQ) + US * u + n + 1):
                        pe.wait_ge(s_u, v)
                    for i in range(2):
                        h = 2 * hh + i
                        last = nc.tensor.matmul(acc[h][0:HW, :], hs[:, (1 - quad.par) * JT + jt, h, :], uv[k][:, i, :],
                                                start=(jt == 0), stop=(jt == JT - 1))
                    last.then_inc(s_pe, 1)

            def step(quad, u):
                if quad.on(u, 1):
                    product0(quad, u)
                if u == 0 and quad.on(u, FIN):
                    back(quad)
                if quad.on(u, QT * BQ):
                    if u == 0:
                        for v in quad.reach(lambda q: q - BQ):
                            pe.wait_ge(s_accfree, v)
                    pe.wait_ge(s_proj, projected(quad, u))
                attend(quad, u, 0, 4)
                if quad.on(u, 1):
                    product1(quad, u)
                attend(quad, u, 4, 6)
                if quad.on(u, -2):
                    transpose_mask(quad, u, 2)
                attend(quad, u, 6, 7)
                if quad.on(u, -2):
                    pack_words(quad, u, 2)
                attend(quad, u, 7, 8)

            for g in range(2):
                transpose_mask(Quad(pe, 0, 0, 0), 0, g)
                pack_words(Quad(pe, 0, 0, 0), 0, g)
            run_quads(pe, step)


def constants():
    import numpy as np
    j = np.arange(P)
    pack = np.zeros((P, WPT), np.float32)
    pack[j, j // WORD] = 2.0 ** (WORD - 1 - j % WORD)
    rows = lambda v, dt: np.tile(np.asarray(v, dt)[None, :], (P, 1))
    return {
        "id16": (np.eye(P, dtype=np.float16), F16),
        "id32": (np.eye(P, dtype=np.float32), F32),
        "pack": (pack, BF16),
        "wordkey": (rows((WORDS - 1 - np.arange(WORDS)) * 2.0 ** WORD, np.float32), F32),
        "nibkey": (rows(16.0 * (NIB - 1 - np.arange(NIB)), np.float32), F32),
        "bitmask": (rows(2 ** (NIB - 1 - np.arange(NIB)), np.int32), I32),
        "colkey": (rows(4.0 - np.arange(NIB), np.float32), F32),
        "rowbase": (rows((np.arange(TILES) // JT + 1) * float(N), np.float32), F32),
    }


_INS = ['x', 'adj', 'L0_gnn_W', 'L0_gnn_b', 'L1_gnn_W', 'L1_gnn_a_src', 'L1_gnn_a_dst', 'L1_gnn_bias',
        'L1_gnn_ln_gamma', 'L1_gnn_ln_beta']
_OUTS = [((B, N, C), 'float32')]


def kernel(**inputs):
    import ml_dtypes
    import numpy as _np
    import concourse.bacc as _bacc
    from concourse import mybir as _mybir
    from concourse.bass_utils import run_bass_kernel_spmd as _run

    nc = _bacc.Bacc("TRN2", target_bir_lowering=False, num_devices=1)
    arrays, args = {}, []
    for name in _INS:
        a = _np.ascontiguousarray(inputs[name])
        arrays[f"in_{name}_dram"] = a
        args.append(nc.dram_tensor(f"in_{name}_dram", a.shape, _mybir.dt.from_np(a.dtype), kind="ExternalInput").ap())
    for name, (a, dt) in constants().items():
        if dt == BF16:
            a = a.astype(ml_dtypes.bfloat16)
        arrays[f"const_{name}_dram"] = a
        args.append(nc.dram_tensor(f"const_{name}_dram", a.shape, dt, kind="ExternalInput").ap())
    for i, (shape, dtype) in enumerate(_OUTS):
        dt = _mybir.dt.from_np(_np.dtype(dtype))
        args.append(nc.dram_tensor(f"out_{i}_dram", shape, dt, kind="ExternalOutput").ap())
    layers_program(nc, *args)
    r = _run(nc, [arrays], core_ids=[0])
    return r.results[0]["out_0_dram"]
```

```python
from contextlib import ExitStack

import concourse.bass as bass
from concourse import mybir

ALU = mybir.AluOpType
ACT = mybir.ActivationFunctionType
AX = mybir.AxisListType
F32 = mybir.dt.float32
F16 = mybir.dt.float16
BF16 = mybir.dt.bfloat16
I32 = mybir.dt.int32
U32 = mybir.dt.uint32
U8 = mybir.dt.uint8

P = 128
B, N, C = 8, 2048, 256
HEADS, HO = 4, 64
HW = HO + 1
S = 25
JT = N // P
TILES = B * JT
QT = 4
IB = QT * P
QUADS = TILES // QT
BQ = JT // QT
RING = 6
WORD = 16
WORDS = N // WORD
WPT = P // WORD
NIB = 4
TOP = 32
CH = 5
CR = S // CH
FIRST = S + 1
HALF = JT // 2
UNITS = JT * 2
US = UNITS // QT
UVB = 4
AHEAD = 3
BIG = 3.0e38
FIN = QT * (BQ + 1)
LN0_EPS = 1e-5
HEAD_EPS = 1e-6
LEAK = 0.01
T = 5
TH = T * HEADS
NEG = -1.0e9
TINY = 1.0e-30
SCORE_SQ = 900.0
SUM_R = 1.0e13


class Quad:

    def __init__(self, eng, q, first, last):
        self.eng, self.q, self.first, self.last, self.par = eng, q, first, last, first // BQ % 2

    def on(self, u, lag):
        here = [0 <= QT * q + u - lag < TILES for q in (self.first, self.last)]
        assert here[0] == here[1]
        return here[0]

    def reach(self, count):
        if count(self.last) <= 0:
            return []
        assert count(self.first) > 0
        return [count(self.q)]


def run_quads(eng, step):
    def quad(q, first, last):
        for u in range(QT):
            step(Quad(eng, q, first, last), u)

    def loop(a, b):
        with eng.Fori(a, b) as q:
            quad(q, a, b - 1)

    quad(0, 0, 0)
    loop(1, BQ - 1)
    quad(BQ - 1, BQ - 1, BQ - 1)
    quad(BQ, BQ, BQ)
    quad(BQ + 1, BQ + 1, BQ + 1)
    loop(BQ + 2, 2 * BQ)
    with eng.Fori(1, B // 2 - 1) as pair:
        for par in range(2):
            with eng.Fori(0, BQ) as k:
                quad(pair * (2 * BQ) + (k + par * BQ), (2 + par) * BQ, (B - 4 + par + 1) * BQ - 1)
    loop(QUADS - 2 * BQ, QUADS - BQ)
    loop(QUADS - BQ, QUADS - 1)
    quad(QUADS - 1, QUADS - 1, QUADS - 1)
    quad(QUADS, QUADS, QUADS)
    loop(QUADS + 1, QUADS + BQ - 1)
    quad(QUADS + BQ - 1, QUADS + BQ - 1, QUADS + BQ - 1)
    quad(QUADS + BQ, QUADS + BQ, QUADS + BQ)
    quad(QUADS + BQ + 1, QUADS + BQ + 1, QUADS + BQ + 1)


def projected(quad, u):
    return QT * quad.q + u - 1 if QT * quad.first + u <= TILES + 1 else TILES


def after(quad, u, ahead):
    return quad.q + (u + ahead) // QT, (u + ahead) % QT


class Chain:

    def __init__(self, eng, sem, between=None):
        self.eng, self.sem, self.n, self.between = eng, sem, 0, between

    def then(self, instruction):
        self.n += 1
        instruction.then_inc(self.sem, 1)
        if self.between:
            self.between(self.n)
        self.eng.wait_ge(self.sem, self.n)

    def end(self):
        self.eng.sem_clear(self.sem)


def layers_program(nc, x, adj, w0, b0, w1, a_src, a_dst, bias1, gamma, beta,
                   c_id16, c_id32, c_pack, c_wordkey, c_nib, c_mask, c_col, c_base, out):
    x_rows = x.rearrange("b n c -> (b n) c")
    adj_rows = adj.rearrange("b n m -> (b n) m")
    out_rows = out.rearrange("b n c -> (b n) c")
    xh_dram = nc.dram_tensor("xh_dram", (B * N, 2 * C), F32).ap()
    r_dram = nc.dram_tensor("r_dram", (HEADS, B * N), F32).ap()
    es_dram = nc.dram_tensor("es_dram", (B * N, TH), F32).ap()
    ed_dram = nc.dram_tensor("ed_dram", (TH, B * N), F32).ap()
    xh_blocks = xh_dram.rearrange("(m i p) c -> p (m i) c", i=QT, p=P)
    out_blocks = out_rows.rearrange("(m i p) c -> p (m i) c", i=QT, p=P)

    ctx = ExitStack()
    with ctx:
        def sb(name, shape, dt):
            return ctx.enter_context(nc.sbuf_tensor(name, shape, dt))

        def ps(name, shape, dt):
            return ctx.enter_context(nc.psum_tensor(name, shape, dt))

        def sem(name):
            return ctx.enter_context(nc.semaphore(name))

        id16 = sb("id16", [P, P], F16)
        id32 = sb("id32", [P, P], F32)
        pack = sb("pack", [P, WPT], BF16)
        wordkey = sb("wordkey", [P, WORDS], F32)
        nibkey = sb("nibkey", [P, NIB], F32)
        bitmask = sb("bitmask", [P, NIB], I32)
        colkey = sb("colkey", [P, NIB], F32)
        w0_sb = sb("w0_sb", [P, 4, C], F32)
        b0_sb = sb("b0_sb", [1, C], F32)
        ones_row = sb("ones_row", [1, P], F32)
        wcat = sb("wcat", [P, 2, C + 2 * HEADS], F32)
        bias_b = sb("bias_b", [P, C], F32)
        gamma_b = sb("gamma_b", [P, C], F32)
        beta_b = sb("beta_b", [P, C], F32)
        eps0 = sb("eps0", [P, 1], F32)
        eps1 = sb("eps1", [P, 1], F32)
        rowbase = sb("rowbase", [P, TILES], F32)
        adj_sb = sb("adj_sb", [P, N], I32)
        mask_sb = sb("mask_sb", [P, N], F16)
        stage = sb("stage", [P, JT, P], BF16)
        maskT = sb("maskT", [P, RING * JT, IB], U8)
        key_a = sb("key_a", [P, WORDS], F32)
        key_b = sb("key_b", [P, WORDS], F32)
        top = sb("top", [P, TOP], F32)
        topi = sb("topi", [P, FIRST], I32)
        part = sb("part", [P, FIRST, NIB], I32)
        high = sb("high", [P, FIRST], I32)
        value = sb("value", [P, FIRST, NIB], F32)
        pad = sb("pad", [P, S], F32)
        lim = [sb(f"lim{p}", [P, 2], F32) for p in range(2)]
        idx = [sb(f"idx{p}", [P, S], U32) for p in range(2)]
        rows = sb("rows", [P, CH, CR * C], F32)
        rmax = sb("rmax", [P, CR * C], F32)
        agg = sb("agg", [P, C], F32)
        xt = [sb(f"xt{p}", [P, C], F32) for p in range(2)]
        xaT = sb("xaT", [P, 4, P], F32)
        r0 = sb("r0", [P, C], F32)
        st0 = sb("st0", [P, 6], F32)
        mv0 = sb("mv0", [P, 2], F32)
        sd0 = sb("sd0", [P, 1], F32)
        rs0 = sb("rs0", [P, 1], F32)
        xh = [sb(f"xh{p}", [P, 2, C], F32) for p in range(2)]
        x1T = sb("x1T", [P, 2, P], F32)
        hs = sb("hs", [P, 2 * JT, HEADS, HW], F32)
        qj = sb("qj", [P, 2 * JT, HEADS], F32)
        dj = sb("dj", [P, HEADS], F32)
        wide = sb("wide", [P, HEADS + 1], F32)
        er = [sb(f"er{p}", [HEADS, P], F32) for p in range(2)]
        rb = sb("rb", [P, 2, HEADS, IB], F32)
        uv = [sb(f"uv{k}", [P, 2, IB], F32) for k in range(UVB)]
        sT = sb("sT", [HW, HEADS, IB], F32)
        rden = sb("rden", [P, QT, HEADS], F32)
        dst = sb("dst", [P, QT, C], F32)
        xr = sb("xr", [P, QT, C], F32)
        sth = sb("sth", [P, QT * HEADS, 6], F32)
        mvh = sb("mvh", [P, QT * HEADS, 2], F32)
        sdh = sb("sdh", [P, QT * HEADS], F32)
        rsh = sb("rsh", [P, QT * HEADS], F32)
        stf = sb("stf", [P, QT, 6], F32)
        mvf = sb("mvf", [P, QT, 2], F32)
        sdf = sb("sdf", [P, QT], F32)
        rsf = sb("rsf", [P, QT], F32)
        tick = sb("tick", [P, 6], F32)

        tiny = sb("tiny", [P, 1], F32)
        minus1 = sb("minus1", [P, 1], F32)
        adj_sq = sb("adj_sq", [P, TILES], F32)
        degree = sb("degree", [P, TILES], F32)
        ed_sq = sb("ed_sq", [P, TILES], F32)
        r_sum = sb("r_sum", [HEADS, TILES], F32)
        redo = sb("redo", [P, 1], I32)

        flat = rows[:].rearrange("p c f -> p (c f)")
        z, zt, ed_row = flat[:, 0:N], flat[:, N:2 * N], flat[:, 2 * N:3 * N]
        rb_flat = rb[:].rearrange("p a h i -> p (a h i)")
        pTs, tmask = rb_flat[:, 0:N], rb_flat[:, N:2 * N]
        hb = hs[:].rearrange("p t h e -> p (t h e)")[:, 0:JT * C]
        a_all = [flat[:, k * TH * HO:(k + 1) * TH * HO] for k in range(2)]
        wst = qj[:].rearrange("p t h -> p (t h)")[:, 0:4 * TH]
        es_all, edT = key_a[:, 0:TH], key_b[0:TH, 0:P]
        d1 = dst[:, 0, :]
        d1_heads = d1.rearrange("p (h e) -> p h e", h=HEADS)

        acc = [ps(f"acc{i}", [P, 512], F32) for i in range(QT)]
        pT = [ps(f"pT{i}", [P, HALF * P], F16) for i in range(2)]
        pA = ps("pA", [P, 512], F32)
        pB = ps("pB", [P, 512], F32)
        p_lin, p_key = pB[:, 0:C], pB[:, 384:384 + WORDS]
        p_h = pB[:, 0:C + 2 * HEADS]
        p_ed = pB[:, C + HEADS:C + 2 * HEADS]
        p_x1T, p_es = pA[:, 0:2 * P], pA[0:HEADS, 2 * P:3 * P]

        s_const = sem("s_const")
        s_go = {e: sem(f"s_go_{e}") for e in ("sp", "act", "pool")}
        s_setup = sem("s_setup")
        s_wa = sem("s_wa")
        s_adj = sem("s_adj")
        s_x = [sem(f"s_xin{p}") for p in range(2)]
        s_mask = sem("s_mask")
        s_T = sem("s_T")
        s_stage = sem("s_stage")
        s_ring = sem("s_ring")
        s_key = sem("s_key")
        s_keyread = sem("s_keyread")
        s_topk = sem("s_topk")
        s_idx = sem("s_idx")
        s_rows = [sem(f"s_rows{c}") for c in range(CH)]
        s_rfree = sem("s_rfree")
        s_maxc = sem("s_maxc")
        s_agg = sem("s_agg")
        s_xaT = sem("s_xaT")
        s_xaE = sem("s_xaE")
        s_lin = sem("s_lin")
        s_r0 = sem("s_r0")
        s_late = sem("s_late")
        s_mv0 = sem("s_mv0")
        s_sd0 = sem("s_sd0")
        s_x1 = sem("s_x1")
        s_xhst = [sem(f"s_xhst{p}") for p in range(2)]
        s_rst = [sem(f"s_rst{p}") for p in range(2)]
        s_x1T = sem("s_x1T")
        s_x1E = sem("s_x1E")
        s_h = sem("s_h")
        s_proj = sem("s_proj")
        s_ed = sem("s_ed")
        s_rb = sem("s_rb")
        s_v = sem("s_v")
        s_u = sem("s_u")
        s_pe = sem("s_pe")
        s_blk = sem("s_blk")
        s_sT = sem("s_sT")
        s_back = sem("s_back")
        s_accfree = sem("s_accfree")
        s_norm = sem("s_norm")
        s_hload = sem("s_hload")
        s_hused = sem("s_hused")
        s_x1load = sem("s_x1load")
        s_fin = sem("s_fin")
        s_mvh = sem("s_mvh")
        s_sdh = sem("s_sdh")
        s_mvf = sem("s_mvf")
        s_sdf = sem("s_sdf")
        s_out = sem("s_out")
        s_st = sem("s_st")
        s_adjread = sem("s_adjread")
        s_good = sem("s_good")
        s_count = sem("s_count")
        s_flag = sem("s_flag")
        s_chain = sem("s_chain")
        s_aload = sem("s_aload")
        s_g1load = sem("s_g1load")
        s_g1T = sem("s_g1T")
        s_g1E = sem("s_g1E")
        s_g1P = sem("s_g1P")
        s_g1S = sem("s_g1S")
        s_g1st = sem("s_g1st")
        s_g2load = sem("s_g2load")
        s_g2ed = sem("s_g2ed")
        s_g2edfree = sem("s_g2edfree")
        s_g2max = sem("s_g2max")
        s_g2p = sem("s_g2p")
        s_g2T = sem("s_g2T")
        s_g2E = sem("s_g2E")
        s_g2d = sem("s_g2d")
        s_g2v = sem("s_g2v")
        s_g2sd = sem("s_g2sd")
        s_g2out = sem("s_g2out")
        s_g2st = sem("s_g2st")

        consts = [(id16[:], c_id16), (id32[:], c_id32), (pack[:], c_pack), (wordkey[:], c_wordkey),
                  (nibkey[:], c_nib), (bitmask[:], c_mask), (colkey[:], c_col),
                  (w0_sb[:], w0.rearrange("(c p) o -> p c o", p=P)),
                  (b0_sb[:], b0.rearrange("(a n) -> a n", a=1)),
                  (bias_b[:], bias1.rearrange("h e -> (h e)").partition_broadcast(P)),
                  (gamma_b[:], gamma.rearrange("h e -> (h e)").partition_broadcast(P)),
                  (beta_b[:], beta.rearrange("h e -> (h e)").partition_broadcast(P)),
                  (rowbase[:], c_base),
                  (dst[:, 0, :].rearrange("p (h e) -> p h e", h=HEADS), a_src[:, 0, :].partition_broadcast(P)),
                  (dst[:, 1, :].rearrange("p (h e) -> p h e", h=HEADS), a_dst[:, 0, :].partition_broadcast(P)),
                  (wcat[:, 0, 0:C].rearrange("p (h e) -> p h e", h=HEADS), w1.rearrange("h (c p) e -> p c h e", p=P)[:, 0]),
                  (wcat[:, 1, 0:C].rearrange("p (h e) -> p h e", h=HEADS), w1.rearrange("h (c p) e -> p c h e", p=P)[:, 1])]
        CONST = 16 * len(consts)


        block = ctx.enter_context(nc.Block())

        @block.sync
        def _(sp):
            for dst_ap, src in consts:
                sp.dma_start(dst_ap, src).then_inc(s_const, 16)
            sp.dma_start(adj_sb[:], adj_rows[0:P, :]).then_inc(s_adj, 16)
            sp.wait_ge(s_adjread, 1)
            sp.dma_start(adj_sb[:], adj_rows[P:2 * P, :]).then_inc(s_adj, 16)

            def step(quad, u):
                s, p = QT * quad.q + u, u % 2
                if quad.on(u, -2):
                    for v in quad.reach(lambda q: QT * q + u + 2):
                        sp.wait_ge(s_adjread, v)
                        sp.sem_inc(s_go["sp"], 1)
                    sp.dma_start(adj_sb[:], adj_rows[bass.ds((s + 2) * P, P), :]).then_inc(s_adj, 16)
                if quad.on(u, 0):
                    for v in quad.reach(lambda q: QT * q + u - 1):
                        sp.wait_ge(s_r0, v)
                        sp.sem_inc(s_go["sp"], 1)
                    sp.dma_start(xt[p][:], x_rows[bass.ds(s * P, P), :]).then_inc(s_x[p], 16)
                if quad.on(u, 2):
                    for v in quad.reach(lambda q: QT * q + u - 1):
                        sp.wait_ge(s_proj, v)
                        sp.sem_inc(s_go["sp"], 1)
                    sp.dma_start(xh_dram[bass.ds((s - 2) * P, P), :], xh[p][:].rearrange("p a c -> p (a c)")).then_inc(s_xhst[p], 16)
                    sp.dma_start(r_dram[:, bass.ds((s - 2) * P, P)], er[p][:]).then_inc(s_rst[p], 16)
                if u == 1 and quad.on(u, QT * BQ - QT):
                    m = quad.q - BQ + 1
                    for o in range(2):
                        for v in quad.reach(lambda q: 32 * (q - BQ + 2)):
                            sp.wait_ge(s_rst[o], v)
                            sp.sem_inc(s_go["sp"], 1)
                    for v in quad.reach(lambda q: UNITS * (q - BQ)):
                        sp.wait_ge(s_v, v)
                        sp.sem_inc(s_go["sp"], 1)
                    dst_rb = rb[:, bass.ds(m % 2, 1), :, :].rearrange("p a h i -> p (a h) i")
                    src_rb = r_dram[:, bass.ds(m * IB, IB)].partition_broadcast(P)
                    sp.dma_start(dst_rb, src_rb).then_inc(s_rb, 16)
                fin = quad.on(u, FIN)
                if u == 0 and quad.on(u, FIN + QT):
                    for v in quad.reach(lambda q: q - BQ - 1):
                        sp.wait_ge(s_out, v)
                        sp.sem_inc(s_go["sp"], 1)
                    sp.dma_start(out_blocks[:, bass.ds((quad.q - BQ - 2) * QT, QT), :], xr[:]).then_inc(s_st, 16)
                if fin and u == 0:
                    for v in quad.reach(lambda q: 16 * (q - BQ - 1)):
                        sp.wait_ge(s_st, v)
                        sp.sem_inc(s_go["sp"], 1)
                    for o in range(2):
                        for v in quad.reach(lambda q: 32 * (q - BQ)):
                            sp.wait_ge(s_xhst[o], v)
                            sp.sem_inc(s_go["sp"], 1)
                    sp.dma_start(xr[:], xh_blocks[:, bass.ds((quad.q - BQ - 1) * QT, QT), C:2 * C]).then_inc(s_hload, 16)
                if fin and u == 2:
                    for v in quad.reach(lambda q: q - BQ):
                        sp.wait_ge(s_hused, v)
                        sp.sem_inc(s_go["sp"], 1)
                    sp.dma_start(xr[:], xh_blocks[:, bass.ds((quad.q - BQ - 1) * QT, QT), 0:C]).then_inc(s_x1load, 16)

            run_quads(sp, step)
            sp.wait_ge(s_st, 16 * QUADS)
            for p in range(2):
                sp.wait_ge(s_xhst[p], 16 * TILES // 2)
                sp.wait_ge(s_rst[p], 16 * TILES // 2)

            sp.wait_ge(s_flag, 1)
            with sp.If(sp.value_load(redo[0:1, 0:1], min_val=0, max_val=1) > 0):
                for k, a in enumerate((a_src, a_dst)):
                    sp.dma_start(a_all[k], a.rearrange("h t e -> (h t e)").partition_broadcast(P)).then_inc(s_aload, 16)
                with sp.Fori(0, TILES) as g:
                    sp.wait_ge(s_g1S, 2 * g + 2)
                    sp.sem_inc(s_go["sp"], 1)
                    sp.dma_start(xr[:, 0, :], xh_dram[bass.ds(g * P, P), 0:C]).then_inc(s_g1load, 16)
                    sp.wait_ge(s_g1S, 2 * g + 4)
                    sp.sem_inc(s_go["sp"], 1)
                    sp.dma_start(es_dram[bass.ds(g * P, P), :], es_all).then_inc(s_g1st, 16)
                    sp.dma_start(ed_dram[:, bass.ds(g * P, P)], edT).then_inc(s_g1st, 16)
                    sp.wait_ge(s_g1st, 32 * g + 32)
                    sp.sem_inc(s_go["sp"], 1)
                with sp.Fori(0, TILES) as g:
                    batch = g // JT
                    sp.dma_start(adj_sb[:], adj_rows[bass.ds(g * P, P), :]).then_inc(s_g2load, 16)
                    sp.dma_start(hb.rearrange("p (j c) -> p j c", c=C),
                                 xh_dram.rearrange("(m p) c -> p m c", p=P)[:, bass.ds(batch * JT, JT), C:2 * C]).then_inc(s_g2load, 16)
                    sp.dma_start(xr[:, 0, :], xh_dram[bass.ds(g * P, P), 0:C]).then_inc(s_g2load, 16)
                    sp.dma_start(xr[:, 1, :], xh_dram[bass.ds(g * P, P), C:2 * C]).then_inc(s_g2load, 16)
                    sp.dma_start(es_all, es_dram[bass.ds(g * P, P), :]).then_inc(s_g2load, 16)
                    for k in range(TH):
                        r = k % T * HEADS + k // T
                        sp.wait_ge(s_g2edfree, TH * g + k + 1)
                        sp.sem_inc(s_go["sp"], 1)
                        sp.dma_start(ed_row, ed_dram[r, bass.ds(batch * N, N)].partition_broadcast(P)).then_inc(s_g2ed, 16)
                    sp.wait_ge(s_g2out, g + 1)
                    sp.sem_inc(s_go["sp"], 1)
                    sp.dma_start(out_rows[bass.ds(g * P, P), :], xr[:, 2, :]).then_inc(s_g2st, 16)
                    sp.wait_ge(s_g2st, 16 * g + 16)
                    sp.sem_inc(s_go["sp"], 1)

        @block.gpsimd
        def _(pool):
            def step(quad, u):
                if not quad.on(u, 0):
                    return
                p = u % 2
                for v in quad.reach(lambda q: QT * q + u + 1):
                    pool.wait_ge(s_idx, v)
                for c in range(CH):
                    for v in quad.reach(lambda q: CH * (QT * q + u) + c + 1):
                        pool.wait_ge(s_rfree, v)
                        pool.sem_inc(s_go["pool"], 1)
                    for r in range(CR):
                        k = c * CR + r
                        nc.gpsimd.indirect_dma_start(
                            rows[:, c, r * C:(r + 1) * C], None, x_rows,
                            bass.IndirectOffsetOnAxis(ap=idx[p][:, k:k + 1], axis=0)).then_inc(s_rows[c], 16)

            run_quads(pool, step)

        @block.scalar
        def _(act):
            act.wait_ge(s_const, CONST)
            act.wait_ge(s_setup, 1)

            def mask(quad, u, g_of):
                for v in quad.reach(lambda q: 16 * (QT * q + u + g_of + 1)):
                    act.wait_ge(s_adj, v)
                for v in quad.reach(lambda q: 2 * (QT * q + u + g_of)):
                    act.wait_ge(s_T, v)
                g = QT * quad.q + u + g_of
                nc.scalar.activation(mask_sb[:], adj_sb[:], ACT.Sign, accum_out=degree[:, bass.ds(g, 1)]).then_inc(s_mask, 1)

            def check(quad, u, g_of):
                for v in quad.reach(lambda q: QT * q + u + g_of):
                    act.wait_ge(s_key, v)
                g = QT * quad.q + u + g_of
                nc.scalar.activation(stage[:].rearrange("p j i -> p (j i)"), adj_sb[:], ACT.Square, scale=2.0, bias=minus1[:],
                                     accum_out=adj_sq[:, bass.ds(g, 1)]).then_inc(s_adjread, 1)

            def transposed(quad, u, g_of):
                qg, ug = after(quad, u, g_of)
                for v in quad.reach(lambda q: QT * q + u + g_of + 1):
                    act.wait_ge(s_adjread, v)
                for hf in range(2):
                    for v in quad.reach(lambda q: 2 * (QT * q + u + g_of) + hf + 1):
                        act.wait_ge(s_T, v)
                    for v in quad.reach(lambda q: QT * q + u + g_of):
                        act.wait_ge(s_key, v)
                    src = pT[hf][:, :].rearrange("p (j i) -> p j i", i=P)
                    nc.scalar.activation(stage[:, hf * HALF:(hf + 1) * HALF, :], src, ACT.Square).then_inc(s_stage, 1)
                    for v in quad.reach(lambda q: q + (u + g_of) // QT + 1):
                        act.wait_ge(s_blk, v)
                    nc.scalar.activation(maskT[:, bass.ds(qg % RING * JT + hf * HALF, HALF), ug * P:(ug + 1) * P],
                                         src, ACT.Square).then_inc(s_ring, 1)

            def scaled(quad, u, n, ahead=0):
                ua = (u + ahead) % QT
                jt, hh, k = QT * ua + n // 2, n % 2, n % UVB
                qa = quad.q + (u + ahead) // QT
                if u + ahead < QT:
                    q_j = lambda h: qj[:, (1 - quad.par) * JT + jt, h:h + 1]
                else:
                    slot = (qa - BQ) // BQ % 2 * JT + jt
                    q_j = lambda h: qj[:, bass.ds(slot, 1), h:h + 1].rearrange("p a h -> p (a h)")
                for v in quad.reach(lambda q: UNITS * (q - BQ) + US * (u + ahead) + n - UVB + 1):
                    act.wait_ge(s_pe, v)
                    act.sem_inc(s_go["act"], 1)
                for i in range(2):
                    h = 2 * hh + i
                    last = nc.scalar.activation(uv[k][:, i, :], rb[:, bass.ds(qa % 2, 1), h, :].rearrange("p a i -> p (a i)"),
                                                ACT.Copy, scale=q_j(h))
                last.then_inc(s_v, 1)

            def scaled_units(quad, u, a, b):
                if quad.on(u, QT * BQ):
                    for n in range(a, b):
                        scaled(quad, u, n)

            def step(quad, u):
                next_attends = quad.on(u, QT * BQ - 1)
                if quad.on(u, QT * BQ) or next_attends:
                    act.wait_ge(s_proj, projected(quad, u))
                if u == 0 and quad.on(u, FIN):
                    for v in quad.reach(lambda q: UNITS * (q - BQ)):
                        act.wait_ge(s_pe, v)
                    for v in quad.reach(lambda q: q - BQ - 1):
                        act.wait_ge(s_back, v)
                    for h in range(HEADS):
                        last = nc.scalar.activation(sT[:, h, :], acc[h][0:HW, :], ACT.Identity, bias=tiny[0:HW, :])
                    last.then_inc(s_sT, 1)
                scaled_units(quad, u, AHEAD, 4)
                if quad.on(u, -2):
                    mask(quad, u, 2)
                if quad.on(u, 1):
                    for v in quad.reach(lambda q: QT * q + u):
                        act.wait_ge(s_mv0, v)
                    nc.scalar.activation(sd0[:], mv0[:, 1:2], ACT.Sqrt, bias=eps0[:]).then_inc(s_sd0, 1)
                if u == 2 and quad.on(u, FIN):
                    for v in quad.reach(lambda q: q - BQ):
                        act.wait_ge(s_mvh, v)
                    nc.scalar.activation(sdh[:], mvh[:, :, 1], ACT.Sqrt, bias=eps1[:]).then_inc(s_sdh, 1)
                scaled_units(quad, u, 4, 6)
                if quad.on(u, 1):
                    project(quad, u)
                if quad.on(u, -2):
                    check(quad, u, 2)
                scaled_units(quad, u, 6, 7)
                if quad.on(u, -2):
                    transposed(quad, u, 2)
                scaled_units(quad, u, 7, 8)
                if u == 3 and quad.on(u, FIN):
                    for v in quad.reach(lambda q: q - BQ):
                        act.wait_ge(s_mvf, v)
                    nc.scalar.activation(sdf[:], mvf[:, :, 1], ACT.Sqrt, bias=eps0[:]).then_inc(s_sdf, 1)
                if next_attends:
                    if u == QT - 1:
                        for v in quad.reach(lambda q: 16 * (q - BQ + 2)):
                            act.wait_ge(s_rb, v)
                            act.sem_inc(s_go["act"], 1)
                    scaled(quad, u, 0, 1)
                if quad.on(u, 0):
                    for v in quad.reach(lambda q: QT * q + u + 1):
                        act.wait_ge(s_xaT, v)
                    for v in quad.reach(lambda q: QT * q + u):
                        act.wait_ge(s_lin, v)
                    nc.scalar.activation(xaT[:, :, :], pA[:, :].rearrange("p (c i) -> p c i", c=4), ACT.Copy).then_inc(s_xaE, 1)
                if next_attends:
                    for n in range(1, AHEAD):
                        scaled(quad, u, n, 1)

            def project(quad, u):
                p = (u - 1) % 2
                qg, ug = after(quad, u, -1)
                for v in quad.reach(lambda q: QT * q + u):
                    act.wait_ge(s_x1T, v)
                nc.scalar.activation(x1T[:, :, :], p_x1T.rearrange("p (c i) -> p c i", c=2), ACT.Copy).then_inc(s_x1E, 1)
                nc.scalar.activation(wide[:, HEADS:HEADS + 1], eps0[:], ACT.Exp)
                for v in quad.reach(lambda q: QT * q + u):
                    act.wait_ge(s_h, v)
                for v in quad.reach(lambda q: UNITS * (q + (u - 1) // QT - BQ)):
                    act.wait_ge(s_pe, v)
                for v in quad.reach(lambda q: 16 * (2 * q + (u - 1) // 2)):
                    act.wait_ge(s_rst[p], v)
                t = qg // BQ % 2 * JT + qg % BQ * QT + ug
                nc.scalar.activation(dj[:], p_ed, ACT.Exp, scale=LEAK).then_inc(s_ed, 1)
                nc.scalar.activation(qj[:, bass.ds(t, 1), :], p_ed.unsqueeze(1), ACT.Exp, scale=1.0 - LEAK)
                nc.scalar.activation(er[p][:], p_es, ACT.Exp, scale=1.0 - LEAK, accum_out=r_sum[:, bass.ds(QT * qg + ug, 1)])
                nc.scalar.activation(wide[:, 0:HEADS], p_ed, ACT.Square, accum_out=ed_sq[:, bass.ds(QT * qg + ug, 1)])
                nc.scalar.activation(xh[p][:, 1, :], pB[:, 0:C], ACT.Copy)
                for v in quad.reach(lambda q: QT * q + u):
                    act.wait_ge(s_ed, v)
                nc.scalar.activation(hs[:, bass.ds(t, 1), :, HO], dj[:].unsqueeze(1), ACT.Copy)
                for h in range(HEADS):
                    last = nc.scalar.activation(hs[:, bass.ds(t, 1), h, 0:HO], pB[:, h * HO:(h + 1) * HO].unsqueeze(1), ACT.Copy,
                                                scale=dj[:, h:h + 1])
                last.then_inc(s_proj, 1)

            for g in range(2):
                mask(Quad(act, 0, 0, 0), 0, g)
                check(Quad(act, 0, 0, 0), 0, g)
                transposed(Quad(act, 0, 0, 0), 0, g)
            run_quads(act, step)

            act.wait_ge(s_flag, 1)
            with act.If(act.value_load(redo[0:1, 0:1], min_val=0, max_val=1) > 0):
                with act.Fori(0, TILES) as g:
                    for h in range(HEADS):
                        act.wait_ge(s_g2max, HEADS * g + h + 1)
                        act.sem_inc(s_go["act"], 1)
                        nc.scalar.activation(z, z, ACT.Exp, bias=rsh[:, 1:2], accum_out=sdh[:, 0:1]).then_inc(s_g2p, 1)
                    act.wait_ge(s_g2v, 2 * g + 1)
                    act.sem_inc(s_go["act"], 1)
                    nc.scalar.activation(sdh[:, 0:HEADS], mvh[:, 0:HEADS, 1], ACT.Sqrt, bias=eps1[:]).then_inc(s_g2sd, 1)
                    act.wait_ge(s_g2v, 2 * g + 2)
                    act.sem_inc(s_go["act"], 1)
                    nc.scalar.activation(sdf[:, 0:1], mvf[:, 0, 1:2], ACT.Sqrt, bias=eps0[:]).then_inc(s_g2sd, 1)

        @block.vector
        def _(dve):
            nc.vector.memset(ones_row[:], 1.0)
            nc.vector.memset(eps0[:], LN0_EPS)
            nc.vector.memset(minus1[:], -1.0)
            nc.vector.memset(tiny[0:HO, :], 0.0)
            nc.vector.memset(tiny[HO:HW, :], TINY)
            nc.vector.memset(eps1[:], HEAD_EPS).then_inc(s_rfree, CH)
            dve.wait_ge(s_const, CONST)
            for c in range(2):
                for k in range(2):
                    nc.vector.tensor_tensor(r0[:], wcat[:, c, 0:C], dst[:, k, :], ALU.mult).then_inc(s_wa, 1)
                    dve.wait_ge(s_wa, 4 * c + 2 * k + 1)
                    nc.vector.tensor_reduce(wcat[:, c, C + HEADS * k:C + HEADS * (k + 1)],
                                            r0[:].rearrange("p (h e) -> p h e", h=HEADS), axis=AX.X, op=ALU.add).then_inc(s_wa, 1)
                    dve.wait_ge(s_wa, 4 * c + 2 * k + 2)
            nc.vector.memset(r0[:, 0:1], 0.0).then_inc(s_blk, RING)
            nc.vector.memset(r0[:, 1:2], 0.0).then_inc(s_setup, 1)

            def top32(ch, keys):
                a, b = key_a[:, 0:keys], key_b[:, 0:keys]
                for k in range(0, TOP, 8):
                    ch.then(nc.vector.max(top[:, k:k + 8], a))
                    if k + 8 < TOP:
                        ch.then(nc.vector.match_replace(b, top[:, k:k + 8], a, 0.0))
                        a, b = b, a

            a3, b3 = (k[:, 0:FIRST * NIB].rearrange("p (t n) -> p t n", n=NIB) for k in (key_a, key_b))

            def search_words(quad, u, g_of, ch):
                for v in quad.reach(lambda q: QT * q + u + g_of + 1):
                    dve.wait_ge(s_key, v)
                ch.then(nc.vector.scalar_tensor_tensor(key_b[:], p_key, 0.0, wordkey[:], ALU.is_gt, ALU.mult))
                ch.then(nc.vector.tensor_tensor(key_a[:], p_key, key_b[:], ALU.add))
                nc.vector.memset(pad[:, 0:1], 0.0).then_inc(s_keyread, 1)
                top32(ch, WORDS)

            def search_nibbles(ch):
                ch.then(nc.vector.tensor_copy(topi[:], top[:, 0:FIRST]))
                nc.vector.tensor_scalar(high[:], topi[:], 10, (WORDS - 1) << 6, ALU.logical_shift_right, ALU.bitwise_and)
                for n in range(NIB):
                    last = nc.vector.tensor_scalar(part[:, :, n], topi[:], WORD - NIB * (n + 1), 15,
                                                   ALU.logical_shift_right, ALU.bitwise_and)
                ch.then(last)
                ch.then(nc.vector.tensor_tensor(value[:], high[:].unsqueeze(2).to_broadcast([P, FIRST, NIB]),
                                                nibkey[:].unsqueeze(1).to_broadcast([P, FIRST, NIB]), ALU.add))
                ch.then(nc.vector.scalar_tensor_tensor(b3, part[:], 0.0, value[:], ALU.is_gt, ALU.mult))
                ch.then(nc.vector.tensor_tensor(a3, part[:], b3, ALU.add))
                top32(ch, FIRST * NIB)

            def search_columns(quad, u, g_of, ch):
                p = (u + g_of) % 2
                g = QT * quad.q + u + g_of
                ch.then(nc.vector.tensor_copy(topi[:], top[:, 0:FIRST]))
                nc.vector.tensor_scalar(high[:], topi[:], 2, N - NIB, ALU.logical_shift_right, ALU.bitwise_and)
                ch.then(nc.vector.tensor_tensor(part[:], topi[:].unsqueeze(2).to_broadcast([P, FIRST, NIB]),
                                                bitmask[:].unsqueeze(1).to_broadcast([P, FIRST, NIB]), ALU.bitwise_and))
                ch.then(nc.vector.tensor_tensor(value[:], high[:].unsqueeze(2).to_broadcast([P, FIRST, NIB]),
                                                colkey[:].unsqueeze(1).to_broadcast([P, FIRST, NIB]), ALU.add))
                ch.then(nc.vector.scalar_tensor_tensor(a3, part[:], 0.0, value[:], ALU.is_gt, ALU.mult))
                top32(ch, FIRST * NIB)
                nc.vector.tensor_scalar(lim[p][:, 0:1], top[:, S:S + 1], 0.0, -BIG, ALU.is_gt, ALU.mult)
                nc.vector.tensor_scalar(lim[p][:, 1:2], top[:, 0:1], 0.0, BIG, ALU.is_gt, ALU.mult)
                ch.then(nc.vector.tensor_scalar(pad[:], top[:, 0:S], 0.0, top[:, 0:1], ALU.is_equal, ALU.mult))
                ch.then(nc.vector.tensor_tensor(pad[:], pad[:], top[:, 0:S], ALU.add))
                ch.then(nc.vector.tensor_scalar(pad[:], pad[:], 1.0, -1.0, ALU.max, ALU.mult))
                nc.vector.tensor_scalar(idx[p][:], pad[:], rowbase[:, bass.ds(g, 1)], None, ALU.add).then_inc(s_idx, 1)
                ch.end()

            def residual(quad, u, part):
                p = (u - 1) % 2
                if part == 0:
                    for v in quad.reach(lambda q: QT * q + u):
                        dve.wait_ge(s_lin, v)
                    nc.vector.scalar_tensor_tensor(r0[:], p_lin, 0.0, xt[p][:], ALU.max, ALU.add).then_inc(s_r0, 1)
                if part == 1:
                    for v in quad.reach(lambda q: QT * q + u):
                        dve.wait_ge(s_r0, v)
                    nc.vector.bn_stats(st0[:], r0[:]).then_inc(s_late, 1)
                if part == 2:
                    dve.wait_ge(s_late, 1)
                    nc.vector.bn_aggr(mv0[:], st0[:]).then_inc(s_late, 1)
                if part == 3:
                    dve.wait_ge(s_late, 2)
                    nc.vector.memset(tick[:, 5:6], 0.0).then_inc(s_mv0, 1)

            def norm0(quad, u, part):
                p = (u - 1) % 2
                if part == 0:
                    for v in quad.reach(lambda q: QT * q + u):
                        dve.wait_ge(s_sd0, v)
                    nc.vector.reciprocal(rs0[:], sd0[:]).then_inc(s_late, 1)
                if part == 1:
                    dve.wait_ge(s_late, 3)
                    dve.sem_clear(s_late)
                    for v in quad.reach(lambda q: 16 * (2 * q + (u - 1) // 2)):
                        dve.wait_ge(s_xhst[p], v)
                    for v in quad.reach(lambda q: QT * q + u - 2):
                        dve.wait_ge(s_x1T, v)
                    nc.vector.tensor_scalar(xh[p][:, 0, :], r0[:], mv0[:, 0:1], rs0[:], ALU.subtract, ALU.mult).then_inc(s_x1, 1)

            def masked(quad, u, n):
                jt, k = QT * u + n // 2, n % UVB
                for v in quad.reach(lambda q: UNITS * (q - BQ) + US * u + n + 1):
                    dve.wait_ge(s_v, v)
                m = maskT[:, bass.ds((quad.q - BQ) % RING * JT + jt, 1), :].to_broadcast([P, 2, IB])
                nc.vector.scalar_tensor_tensor(uv[k][:], uv[k][:], 1.0, m, ALU.max, ALU.mult).then_inc(s_u, 1)
                if u == QT - 1 and n == US - 1:
                    nc.vector.memset(tick[:, 4:5], 0.0).then_inc(s_blk, 1)

            def maximum(quad, u, c):
                if c == 1:
                    for v in quad.reach(lambda q: 16 * CR * (QT * q + u + 1)):
                        dve.wait_ge(s_rows[0], v)
                else:
                    for v in quad.reach(lambda q: CH * (QT * q + u + 1) + c):
                        dve.wait_ge(s_rfree, v)
                for v in quad.reach(lambda q: 16 * CR * (QT * q + u + 1)):
                    dve.wait_ge(s_rows[c], v)
                before = rows[:, 0, :] if c == 1 else rmax[:]
                nc.vector.tensor_tensor(rmax[:], before, rows[:, c, :], ALU.max).then_inc(s_rfree, 2 if c == 1 else 1)

            def aggregate(quad, u):
                for v in quad.reach(lambda q: CH * (QT * q + u + 2)):
                    dve.wait_ge(s_rfree, v)
                for v in quad.reach(lambda q: QT * q + u):
                    dve.wait_ge(s_xaT, v)
                ch = Chain(dve, s_maxc)
                ch.then(nc.vector.tensor_reduce(agg[:], rmax[:].rearrange("p (r f) -> p f r", f=C), axis=AX.X, op=ALU.max))
                nc.vector.tensor_scalar(agg[:], agg[:], lim[u % 2][:, 0:1], lim[u % 2][:, 1:2], ALU.max, ALU.min).then_inc(s_agg, 1)
                ch.end()

            def divide(quad):
                for v in quad.reach(lambda q: q - BQ):
                    dve.wait_ge(s_back, v)
                for v in quad.reach(lambda q: q - BQ - 1):
                    dve.wait_ge(s_out, v)
                ch = Chain(dve, s_norm)
                sums = [a[:, 0:HEADS * HW].rearrange("p (h e) -> p h e", h=HEADS) for a in acc]
                for i in range(QT):
                    last = nc.vector.reciprocal(rden[:, i, :], sums[i][:, :, HO])
                ch.then(last)
                for i in range(QT):
                    last = nc.vector.tensor_tensor(dst[:, i, :].rearrange("p (h e) -> p h e", h=HEADS), sums[i][:, :, 0:HO],
                                                   rden[:, i, :].unsqueeze(2).to_broadcast([P, HEADS, HO]), ALU.mult)
                ch.then(last)
                ch.end()
                nc.vector.memset(tick[:, 3:4], 0.0).then_inc(s_accfree, 1)

            heads = dst[:].rearrange("p i (h e) -> p (i h) e", h=HEADS)

            def per_head(a):
                return a.unsqueeze(2).to_broadcast([P, QT * HEADS, HO])

            def per_column(a):
                return a[:].unsqueeze(1).to_broadcast([P, QT, C])

            def finish_heads(quad, part):
                if part == 0:
                    nc.vector.tensor_tensor(dst[:], dst[:], per_column(bias_b), ALU.add).then_inc(s_fin, 1)
                if part == 1:
                    dve.wait_ge(s_fin, 1)
                    for v in quad.reach(lambda q: 16 * (q - BQ)):
                        dve.wait_ge(s_hload, v)
                    nc.vector.scalar_tensor_tensor(dst[:], dst[:], 0.0, xr[:], ALU.max, ALU.add).then_inc(s_fin, 1)
                if part == 2:
                    dve.wait_ge(s_fin, 2)
                    nc.vector.memset(tick[:, 0:1], 0.0).then_inc(s_hused, 1)
                    for h in range(QT * HEADS):
                        last = nc.vector.bn_stats(sth[:, h, :], heads[:, h, :])
                    last.then_inc(s_fin, 1)
                if part == 3:
                    dve.wait_ge(s_fin, 3)
                    for h in range(QT * HEADS):
                        last = nc.vector.bn_aggr(mvh[:, h, :], sth[:, h, :])
                    last.then_inc(s_fin, 1)
                if part == 4:
                    dve.wait_ge(s_fin, 4)
                    dve.sem_clear(s_fin)
                    nc.vector.memset(tick[:, 1:2], 0.0).then_inc(s_mvh, 1)

            def finish_norm(quad, part):
                if part == 0:
                    nc.vector.tensor_tensor(heads, heads, per_head(mvh[:, :, 0]), ALU.subtract).then_inc(s_fin, 1)
                if part == 1:
                    for v in quad.reach(lambda q: q - BQ):
                        dve.wait_ge(s_sdh, v)
                    nc.vector.reciprocal(rsh[:], sdh[:]).then_inc(s_fin, 1)
                if part == 2:
                    dve.wait_ge(s_fin, 2)
                    nc.vector.tensor_tensor(heads, heads, per_head(rsh[:]), ALU.mult).then_inc(s_fin, 1)
                if part == 3:
                    dve.wait_ge(s_fin, 3)
                    nc.vector.tensor_tensor(dst[:], dst[:], per_column(gamma_b), ALU.mult).then_inc(s_fin, 1)
                if part == 4:
                    dve.wait_ge(s_fin, 4)
                    nc.vector.tensor_tensor(dst[:], dst[:], per_column(beta_b), ALU.add).then_inc(s_fin, 1)
                if part == 5:
                    dve.wait_ge(s_fin, 5)
                    dve.sem_clear(s_fin)

            def finish_sums(quad, part):
                if part == 0:
                    for v in quad.reach(lambda q: 16 * (q - BQ)):
                        dve.wait_ge(s_x1load, v)
                    nc.vector.tensor_tensor(dst[:], dst[:], xr[:], ALU.add).then_inc(s_fin, 1)
                if part == 1:
                    dve.wait_ge(s_fin, 1)
                    for i in range(QT):
                        last = nc.vector.bn_stats(stf[:, i, :], dst[:, i, :])
                    last.then_inc(s_fin, 1)
                if part == 2:
                    dve.wait_ge(s_fin, 2)
                    for i in range(QT):
                        last = nc.vector.bn_aggr(mvf[:, i, :], stf[:, i, :])
                    last.then_inc(s_fin, 1)
                if part == 3:
                    dve.wait_ge(s_fin, 3)
                    dve.sem_clear(s_fin)
                    nc.vector.memset(tick[:, 2:3], 0.0).then_inc(s_mvf, 1)

            def finish_rows(quad):
                ch = Chain(dve, s_fin)
                for v in quad.reach(lambda q: q - BQ):
                    dve.wait_ge(s_sdf, v)
                ch.then(nc.vector.reciprocal(rsf[:], sdf[:]))
                for i in range(QT):
                    last = nc.vector.tensor_scalar(xr[:, i, :], dst[:, i, :], mvf[:, i, 0:1], rsf[:, i:i + 1], ALU.subtract, ALU.mult)
                last.then_inc(s_out, 1)
                ch.end()

            LINKS = 35
            UNIT_AT = (2, 4, 6, 14, 22, 31)
            CHUNK_AT = (12, 19, 26)
            RESIDUAL_AT = (7, 8, 10, 11)
            DIVIDE_AT = 6
            NORM_AT = (15, 17)
            FINISH_AT = (16, 18, 20, 24, 27, 29)

            def step(quad, u):
                ahead, behind, att, gather, fin = (quad.on(u, lag) for lag in (-1, 1, QT * BQ, 0, FIN))

                def between(place):
                    if att and place in UNIT_AT:
                        masked(quad, u, 1 + UNIT_AT.index(place))
                    if behind and place in RESIDUAL_AT:
                        residual(quad, u, RESIDUAL_AT.index(place))
                    if fin and u == 0 and place == DIVIDE_AT:
                        divide(quad)
                    if behind and place in NORM_AT:
                        norm0(quad, u, NORM_AT.index(place))
                    if gather and place in CHUNK_AT:
                        maximum(quad, u, 1 + CHUNK_AT.index(place))
                    if fin and place in FINISH_AT and u > 0:
                        (finish_heads, finish_norm, finish_sums)[u - 1](quad, FINISH_AT.index(place))

                if att:
                    masked(quad, u, 0)
                if ahead:
                    search = Chain(dve, s_topk, between)
                    search_words(quad, u, 1, search)
                    search_nibbles(search)
                    search_columns(quad, u, 1, search)
                    assert search.n == LINKS
                else:
                    for place in range(1, LINKS + 1):
                        between(place)
                if gather:
                    maximum(quad, u, CH - 1)
                    aggregate(quad, u)
                if att:
                    masked(quad, u, US - 1)
                if fin and u == QT - 1:
                    finish_rows(quad)

            def general_tile(g):
                ch = Chain(dve, s_chain)
                dve.wait_ge(s_g2load, 80 * g + 80)
                for h in range(HEADS):
                    for t in range(T):
                        r = t * HEADS + h
                        ch.then(nc.vector.tensor_scalar(tmask, adj_sb[:], float(t + 1), None, ALU.is_equal))
                        dve.wait_ge(s_g2ed, 16 * TH * g + 16 * (h * T + t + 1))
                        ch.then(nc.vector.scalar_tensor_tensor(zt if t else z, ed_row, es_all[:, r:r + 1], tmask, ALU.add, ALU.mult))
                        nc.vector.memset(tick[:, 0:1], 0.0).then_inc(s_g2edfree, 1)
                        if t:
                            ch.then(nc.vector.tensor_tensor(z, z, zt, ALU.add))
                    ch.then(nc.vector.scalar_tensor_tensor(z, z, LEAK, z, ALU.mult, ALU.max))
                    ch.then(nc.vector.tensor_scalar(tmask, adj_sb[:], 0.0, NEG, ALU.is_equal, ALU.mult))
                    ch.then(nc.vector.tensor_tensor(z, z, tmask, ALU.add))
                    ch.then(nc.vector.tensor_reduce(rsh[:, 0:1], z, axis=AX.X, op=ALU.max))
                    nc.vector.tensor_scalar(rsh[:, 1:2], rsh[:, 0:1], -1.0, None, ALU.mult).then_inc(s_g2max, 1)
                    dve.wait_ge(s_g2T, HEADS * g + h + 1)
                    for i in range(QT):
                        last = nc.vector.tensor_copy(pTs[:, i * 512:(i + 1) * 512], acc[i][:])
                    last.then_inc(s_g2E, 1)
                    dve.wait_ge(s_g2p, HEADS * g + h + 1)
                    dve.wait_ge(s_g2d, HEADS * g + h + 1)
                    ch.then(nc.vector.reciprocal(rsh[:, 2:3], sdh[:, 0:1]))
                    ch.then(nc.vector.tensor_scalar(d1[:, h * HO:(h + 1) * HO], pA[:, 0:HO], rsh[:, 2:3], None, ALU.mult))
                ch.then(nc.vector.tensor_tensor(d1, d1, bias_b[:], ALU.add))
                ch.then(nc.vector.scalar_tensor_tensor(d1, d1, 0.0, xr[:, 1, :], ALU.max, ALU.add))
                for h in range(HEADS):
                    last = nc.vector.bn_stats(sth[:, h, :], d1_heads[:, h, :])
                ch.then(last)
                for h in range(HEADS):
                    last = nc.vector.bn_aggr(mvh[:, h, :], sth[:, h, :])
                ch.then(last)
                nc.vector.memset(tick[:, 1:2], 0.0).then_inc(s_g2v, 1)
                ch.then(nc.vector.tensor_tensor(d1_heads, d1_heads, mvh[:, 0:HEADS, 0].unsqueeze(2).to_broadcast([P, HEADS, HO]),
                                                ALU.subtract))
                dve.wait_ge(s_g2sd, 2 * g + 1)
                ch.then(nc.vector.reciprocal(rsh[:, 4:4 + HEADS], sdh[:, 0:HEADS]))
                ch.then(nc.vector.tensor_tensor(d1_heads, d1_heads, rsh[:, 4:4 + HEADS].unsqueeze(2).to_broadcast([P, HEADS, HO]),
                                                ALU.mult))
                ch.then(nc.vector.tensor_tensor(d1, d1, gamma_b[:], ALU.mult))
                ch.then(nc.vector.tensor_tensor(d1, d1, beta_b[:], ALU.add))
                ch.then(nc.vector.tensor_tensor(d1, d1, xr[:, 0, :], ALU.add))
                ch.then(nc.vector.bn_stats(stf[:, 0, :], d1))
                ch.then(nc.vector.bn_aggr(mvf[:, 0, :], stf[:, 0, :]))
                nc.vector.memset(tick[:, 1:2], 0.0).then_inc(s_g2v, 1)
                dve.wait_ge(s_g2sd, 2 * g + 2)
                ch.then(nc.vector.reciprocal(rsf[:, 0:1], sdf[:, 0:1]))
                nc.vector.tensor_scalar(xr[:, 2, :], d1, mvf[:, 0, 0:1], rsf[:, 0:1], ALU.subtract, ALU.mult).then_inc(s_g2out, 1)
                ch.end()

            search = Chain(dve, s_topk)
            search_words(Quad(dve, 0, 0, 0), 0, 0, search)
            search_nibbles(search)
            search_columns(Quad(dve, 0, 0, 0), 0, 0, search)
            run_quads(dve, step)

            ch = Chain(dve, s_chain)
            dve.wait_ge(s_adjread, TILES)
            dve.wait_ge(s_mask, TILES)
            dve.wait_ge(s_proj, TILES)
            dve.wait_ge(s_h, TILES)
            nc.vector.memset(x1T[:, 0, :], 1.0)
            ch.then(nc.vector.tensor_scalar(key_a[:], adj_sq[:], float(N), None, ALU.is_equal))
            for stat, limit, op in ((degree[:], 1.0, ALU.is_ge), (ed_sq[:], SCORE_SQ, ALU.is_le), (r_sum[:], SUM_R, ALU.is_le)):
                n = HEADS if op == ALU.is_le and limit == SUM_R else P
                ch.then(nc.vector.tensor_scalar(key_b[0:n, :], stat, limit, None, op))
                ch.then(nc.vector.tensor_tensor(key_a[0:n, :], key_a[0:n, :], key_b[0:n, :], ALU.mult))
            nc.vector.memset(tick[:, 0:1], 0.0).then_inc(s_good, 1)
            dve.wait_ge(s_count, 1)
            ch.then(nc.vector.tensor_scalar(key_b[:], pA[:, 0:TILES], float(P), None, ALU.is_equal))
            ch.then(nc.vector.tensor_reduce(rs0[:], key_b[:], axis=AX.X, op=ALU.min))
            nc.vector.tensor_scalar(redo[:], rs0[:], 0.0, None, ALU.is_equal).then_inc(s_flag, 1)
            ch.end()
            dve.wait_ge(s_flag, 1)
            with dve.If(dve.value_load(redo[0:1, 0:1], min_val=0, max_val=1) > 0):
                dve.wait_ge(s_aload, 32)
                ch = Chain(dve, s_chain)
                for c in range(2):
                    for k in range(2):
                        for t in range(T):
                            vec = a_all[k].rearrange("p (h t e) -> p h t e", h=HEADS, t=T)[:, :, t, :]
                            w = wcat[:, c, 0:C].rearrange("p (h e) -> p h e", h=HEADS)
                            at = ((c * 2 + k) * T + t) * HEADS
                            ch.then(nc.vector.tensor_tensor(r0[:].rearrange("p (h e) -> p h e", h=HEADS), w, vec, ALU.mult))
                            ch.then(nc.vector.tensor_reduce(wst[:, at:at + HEADS], r0[:].rearrange("p (h e) -> p h e", h=HEADS),
                                                            axis=AX.X, op=ALU.add))
                ch.end()
                nc.vector.memset(tick[:, 1:2], 0.0).then_inc(s_g1S, 2)
                nc.vector.memset(tick[:, 2:3], 0.0).then_inc(s_g2edfree, 1)
                with dve.Fori(0, TILES) as g:
                    dve.wait_ge(s_g1T, g + 1)
                    nc.vector.tensor_copy(x1T[:].rearrange("p c i -> p (c i)"), pA[:, 0:2 * P]).then_inc(s_g1E, 1)
                    dve.wait_ge(s_g1P, g + 1)
                    nc.vector.tensor_copy(es_all, pB[:, 0:TH]).then_inc(s_g1S, 1)
                    nc.vector.tensor_copy(edT, pA[0:TH, 2 * P:3 * P]).then_inc(s_g1S, 1)
                with dve.Fori(0, TILES) as g:
                    general_tile(g)

        @block.tensor
        def _(pe):
            pe.wait_ge(s_const, CONST)
            pe.wait_ge(s_setup, 1)

            def transpose_mask(quad, u, g_of):
                for v in quad.reach(lambda q: QT * q + u + g_of + 1):
                    pe.wait_ge(s_mask, v)
                for hf in range(2):
                    for v in quad.reach(lambda q: 2 * (QT * q + u + g_of - 1) + hf + 1):
                        pe.wait_ge(s_ring, v)
                    for j in range(HALF):
                        jt = hf * HALF + j
                        last = nc.tensor.transpose(pT[hf][:, j * P:(j + 1) * P], mask_sb[:, jt * P:(jt + 1) * P], id16[:])
                    last.then_inc(s_T, 1)

            def pack_words(quad, u, g_of):
                for v in quad.reach(lambda q: 2 * (QT * q + u + g_of + 1)):
                    pe.wait_ge(s_stage, v)
                for v in quad.reach(lambda q: QT * q + u + g_of):
                    pe.wait_ge(s_keyread, v)
                for v in quad.reach(lambda q: QT * q + u + g_of - 2):
                    pe.wait_ge(s_proj, v)
                for jt in range(JT):
                    last = nc.tensor.matmul(p_key[:, jt * WPT:(jt + 1) * WPT], stage[:, jt, :], pack[:], start=True, stop=True)
                last.then_inc(s_key, 1)

            def back(quad):
                for v in quad.reach(lambda q: q - BQ):
                    pe.wait_ge(s_sT, v)
                for i in range(QT):
                    for h in range(HEADS):
                        last = nc.tensor.transpose(acc[i][:, h * HW:(h + 1) * HW], sT[:, h, i * P:(i + 1) * P], id32[0:HW, 0:HW])
                last.then_inc(s_back, 1)

            def transpose_xa(quad, u):
                p = u % 2
                for v in quad.reach(lambda q: QT * q + u + 1):
                    pe.wait_ge(s_agg, v)
                for v in quad.reach(lambda q: 16 * (2 * q + u // 2 + 1)):
                    pe.wait_ge(s_x[p], v)
                for v in quad.reach(lambda q: QT * q + u):
                    pe.wait_ge(s_proj, v)
                for c in range(4):
                    src = (xt[p] if c < 2 else agg)[:, c % 2 * P:(c % 2 + 1) * P]
                    last = nc.tensor.transpose(pA[:, c * P:(c + 1) * P], src, id32[:])
                last.then_inc(s_xaT, 1)

            def product0(quad, u):
                if quad.on(u, -1):
                    for v in quad.reach(lambda q: QT * q + u + 2):
                        pe.wait_ge(s_keyread, v)
                for v in quad.reach(lambda q: QT * q + u):
                    pe.wait_ge(s_xaE, v)
                for c in range(4):
                    nc.tensor.matmul(p_lin, xaT[:, c, :], w0_sb[:, c, :], start=(c == 0), stop=False)
                nc.tensor.matmul(p_lin, ones_row[:], b0_sb[:], start=False, stop=True).then_inc(s_lin, 1)

            def product1(quad, u):
                p = (u - 1) % 2
                for v in quad.reach(lambda q: QT * q + u):
                    pe.wait_ge(s_x1, v)
                for c in range(2):
                    last = nc.tensor.transpose(p_x1T[:, c * P:(c + 1) * P], xh[p][:, 0, c * P:(c + 1) * P], id32[:])
                last.then_inc(s_x1T, 1)
                for v in quad.reach(lambda q: QT * q + u):
                    pe.wait_ge(s_x1E, v)
                for c in range(2):
                    nc.tensor.matmul(p_h, x1T[:, c, :], wcat[:, c, :], start=(c == 0), stop=(c == 1))
                for c in range(2):
                    last = nc.tensor.matmul(p_es, wcat[:, c, C:C + HEADS], x1T[:, c, :], start=(c == 0), stop=(c == 1))
                last.then_inc(s_h, 1)

            def attend(quad, u, a, b):
                if not quad.on(u, QT * BQ):
                    return
                for n in range(a, b):
                    jt, hh, k = QT * u + n // 2, n % 2, n % UVB
                    for v in quad.reach(lambda q: UNITS * (q - BQ) + US * u + n + 1):
                        pe.wait_ge(s_u, v)
                    for i in range(2):
                        h = 2 * hh + i
                        last = nc.tensor.matmul(acc[h][0:HW, :], hs[:, (1 - quad.par) * JT + jt, h, :], uv[k][:, i, :],
                                                start=(jt == 0), stop=(jt == JT - 1))
                    last.then_inc(s_pe, 1)

            def step(quad, u):
                if u == 0 and quad.on(u, FIN):
                    back(quad)
                if quad.on(u, 1):
                    product0(quad, u)
                if quad.on(u, QT * BQ):
                    if u == 0:
                        for v in quad.reach(lambda q: q - BQ):
                            pe.wait_ge(s_accfree, v)
                    pe.wait_ge(s_proj, projected(quad, u))
                attend(quad, u, 0, 4)
                if quad.on(u, 1):
                    product1(quad, u)
                attend(quad, u, 4, 6)
                if quad.on(u, -2):
                    transpose_mask(quad, u, 2)
                attend(quad, u, 6, 7)
                if quad.on(u, -2):
                    pack_words(quad, u, 2)
                if quad.on(u, 0):
                    transpose_xa(quad, u)
                attend(quad, u, 7, 8)

            for g in range(2):
                transpose_mask(Quad(pe, 0, 0, 0), 0, g)
                pack_words(Quad(pe, 0, 0, 0), 0, g)
            run_quads(pe, step)

            pe.wait_ge(s_good, 1)
            nc.tensor.matmul(pA[:, 0:TILES], x1T[:, 0, :], key_a[:], start=True, stop=True).then_inc(s_count, 1)
            pe.wait_ge(s_flag, 1)
            with pe.If(pe.value_load(redo[0:1, 0:1], min_val=0, max_val=1) > 0):
                with pe.Fori(0, TILES) as g:
                    pe.wait_ge(s_g1load, 16 * g + 16)
                    for c in range(2):
                        last = nc.tensor.transpose(pA[:, c * P:(c + 1) * P], xr[:, 0, c * P:(c + 1) * P], id32[:])
                    last.then_inc(s_g1T, 1)
                    pe.wait_ge(s_g1E, g + 1)
                    for c in range(2):
                        nc.tensor.matmul(pB[:, 0:TH], x1T[:, c, :], wst[:, 2 * c * TH:(2 * c + 1) * TH], start=(c == 0), stop=(c == 1))
                    for c in range(2):
                        last = nc.tensor.matmul(pA[0:TH, 2 * P:3 * P], wst[:, (2 * c + 1) * TH:(2 * c + 2) * TH], x1T[:, c, :],
                                                start=(c == 0), stop=(c == 1))
                    last.then_inc(s_g1P, 1)
                with pe.Fori(0, TILES) as g:
                    for h in range(HEADS):
                        pe.wait_ge(s_g2p, HEADS * g + h + 1)
                        for j in range(JT):
                            last = nc.tensor.transpose(acc[j // QT][:, j % QT * P:(j % QT + 1) * P], z[:, j * P:(j + 1) * P], id32[:])
                        last.then_inc(s_g2T, 1)
                        pe.wait_ge(s_g2E, HEADS * g + h + 1)
                        for j in range(JT):
                            last = nc.tensor.matmul(pA[:, 0:HO], pTs[:, j * P:(j + 1) * P], hb[:, j * C + h * HO:j * C + (h + 1) * HO],
                                                    start=(j == 0), stop=(j == JT - 1))
                        last.then_inc(s_g2d, 1)


def constants():
    import numpy as np
    j = np.arange(P)
    pack = np.zeros((P, WPT), np.float32)
    pack[j, j // WORD] = 2.0 ** (WORD - 1 - j % WORD)
    rows = lambda v, dt: np.tile(np.asarray(v, dt)[None, :], (P, 1))
    return {
        "id16": (np.eye(P, dtype=np.float16), F16),
        "id32": (np.eye(P, dtype=np.float32), F32),
        "pack": (pack, BF16),
        "wordkey": (rows((WORDS - 1 - np.arange(WORDS)) * 2.0 ** WORD, np.float32), F32),
        "nibkey": (rows(16.0 * (NIB - 1 - np.arange(NIB)), np.float32), F32),
        "bitmask": (rows(2 ** (NIB - 1 - np.arange(NIB)), np.int32), I32),
        "colkey": (rows(4.0 - np.arange(NIB), np.float32), F32),
        "rowbase": (rows((np.arange(TILES) // JT + 1) * float(N), np.float32), F32),
    }


_INS = ['x', 'adj', 'L0_gnn_W', 'L0_gnn_b', 'L1_gnn_W', 'L1_gnn_a_src', 'L1_gnn_a_dst', 'L1_gnn_bias',
        'L1_gnn_ln_gamma', 'L1_gnn_ln_beta']
_OUTS = [((B, N, C), 'float32')]


def kernel(**inputs):
    import ml_dtypes
    import numpy as _np
    import concourse.bacc as _bacc
    from concourse import mybir as _mybir
    from concourse.bass_utils import run_bass_kernel_spmd as _run

    nc = _bacc.Bacc("TRN2", target_bir_lowering=False, num_devices=1)
    arrays, args = {}, []
    for name in _INS:
        a = _np.ascontiguousarray(inputs[name])
        arrays[f"in_{name}_dram"] = a
        args.append(nc.dram_tensor(f"in_{name}_dram", a.shape, _mybir.dt.from_np(a.dtype), kind="ExternalInput").ap())
    for name, (a, dt) in constants().items():
        if dt == BF16:
            a = a.astype(ml_dtypes.bfloat16)
        arrays[f"const_{name}_dram"] = a
        args.append(nc.dram_tensor(f"const_{name}_dram", a.shape, dt, kind="ExternalInput").ap())
    for i, (shape, dtype) in enumerate(_OUTS):
        dt = _mybir.dt.from_np(_np.dtype(dtype))
        args.append(nc.dram_tensor(f"out_{i}_dram", shape, dt, kind="ExternalOutput").ap())
    layers_program(nc, *args)
    r = _run(nc, [arrays], core_ids=[0])
    return r.results[0]["out_0_dram"]
```
